# Optimizing a Trainium2 kernel written in Bass

```python
import numpy as np
import jax
import jax.numpy as jnp

def _softmax(x, axis=-1):
    return jax.nn.softmax(x, axis=axis)

def _gelu(x):
    return jax.nn.gelu(x, approximate=True)

def _silu(x):
    return jax.nn.silu(x)

def _sigmoid(x):
    return jax.nn.sigmoid(x)

def _layernorm(x, axis=-1, eps=1e-05):
    m = jnp.mean(x, axis=axis, keepdims=True)
    v = jnp.var(x, axis=axis, keepdims=True)
    return (x - m) / jnp.sqrt(v + eps)

def _scatter_add(tgt, idx, src, axis=0):
    return tgt.at[idx].add(src)

def _segment_sum(src, seg, n):
    return jax.ops.segment_sum(src, seg, n)
kernel_name = 'mk_metaformer_d1_conv_nhwc256_r4_9af472'

def setup_inputs(seed: int=0):
    np.random.seed(seed)
    _w = jnp.asarray

    def _rec_inputs():
        import jax
        import jax.numpy as jnp
        _gk = jax.random.key(seed)
        x = 7.22e-05 + 1 * jax.random.normal(jax.random.fold_in(_gk, 1), (2, 32, 32, 64), jnp.float32)
        return x
    x = _rec_inputs()

    def _L0_conv_setup():
        import jax, jax.numpy as jnp
        import numpy as np
        B, HIMG, WIMG, C = (2, 32, 32, 64)
        NH, HD = (8, 32)
        WH, WW = (8, 8)
        P = WH * WW
        NQK = 5
        S = 1 + HD + HD
        EPS = 1e-05

        def _spatial(intrinsic):
            ii = jnp.arange(WH)
            jj = jnp.arange(WW)
            ri = ii[:, None] - ii[None, :] + WH - 1
            rj = jj[:, None] - jj[None, :] + WW - 1
            rel = intrinsic[:, ri[:, None, :, None], rj[None, :, None, :], :]
            rel = rel.transpose(1, 2, 0, 3, 4, 5).reshape(P, NH, P, S)
            return (rel[..., 0], rel[..., 1:1 + HD], rel[..., 1 + HD:])
        key = jax.random.key(seed)
        ks = jax.random.split(key, 6)
        obtained = NH * HD * NQK
        bound = np.sqrt(6.0 / (P * 1 + P))
        return {'x': jax.random.normal(ks[0], (B, HIMG, WIMG, C), jnp.float32), 'W_prep': jax.random.normal(ks[1], (C, obtained), jnp.float32) * (1.0 / np.sqrt(C)), 'b_prep': jnp.zeros((obtained,), jnp.float32), 'intrinsic': jax.random.uniform(ks[2], (NH, 2 * WH - 1, 2 * WW - 1, S), jnp.float32, minval=-bound, maxval=bound), 'W_fin': jax.random.normal(ks[3], (NH * HD, C), jnp.float32) * (1.0 / np.sqrt(NH * HD)), 'b_fin': jnp.zeros((C,), jnp.float32)}
    _L0_conv_all = _L0_conv_setup()
    _L0_conv_in = {k: v for k, v in _L0_conv_all.items() if k in ('W_prep', 'b_prep', 'intrinsic', 'W_fin', 'b_fin')}
    del _L0_conv_all

    def _L0_ffn_setup():
        import jax, jax.numpy as jnp
        import numpy as np
        TOP_K = 2
        LN_EPS = 1e-05
        key = jax.random.key(seed)
        ks = jax.random.split(key, 8)
        B, S, D, E, H = (16, 256, 64, 8, 256)
        x = jax.random.normal(ks[0], (B, S, D), dtype=jnp.float32)
        Wr = jax.random.normal(ks[1], (D, E), dtype=jnp.float32) * 0.1
        br = jnp.zeros((E,), dtype=jnp.float32)
        ln_g = jnp.ones((E, D), dtype=jnp.float32)
        ln_b = jnp.zeros((E, D), dtype=jnp.float32)
        W1 = jax.random.normal(ks[2], (E, D, H), dtype=jnp.float32) * (1.0 / np.sqrt(D))
        b1 = jnp.zeros((E, H), dtype=jnp.float32)
        W2 = jax.random.normal(ks[3], (E, H, D), dtype=jnp.float32) * (1.0 / np.sqrt(H))
        b2 = jnp.zeros((E, D), dtype=jnp.float32)
        return {'x': x, 'Wr': Wr, 'br': br, 'ln_g': ln_g, 'ln_b': ln_b, 'W1': W1, 'b1': b1, 'W2': W2, 'b2': b2}
    _L0_ffn_all = _L0_ffn_setup()
    _L0_ffn_in = {k: v for k, v in _L0_ffn_all.items() if k in ('Wr', 'br', 'ln_g', 'ln_b', 'W1', 'b1', 'W2', 'b2')}
    del _L0_ffn_all
    return {'x': x, 'L0_conv_W_prep': _L0_conv_in['W_prep'], 'L0_conv_b_prep': _L0_conv_in['b_prep'], 'L0_conv_intrinsic': _L0_conv_in['intrinsic'], 'L0_conv_W_fin': _L0_conv_in['W_fin'], 'L0_conv_b_fin': _L0_conv_in['b_fin'], 'L0_ffn_Wr': _L0_ffn_in['Wr'], 'L0_ffn_br': _L0_ffn_in['br'], 'L0_ffn_ln_g': _L0_ffn_in['ln_g'], 'L0_ffn_ln_b': _L0_ffn_in['ln_b'], 'L0_ffn_W1': _L0_ffn_in['W1'], 'L0_ffn_b1': _L0_ffn_in['b1'], 'L0_ffn_W2': _L0_ffn_in['W2'], 'L0_ffn_b2': _L0_ffn_in['b2']}

def reference(x, L0_conv_W_prep, L0_conv_b_prep, L0_conv_intrinsic, L0_conv_W_fin, L0_conv_b_fin, L0_ffn_Wr, L0_ffn_br, L0_ffn_ln_g, L0_ffn_ln_b, L0_ffn_W1, L0_ffn_b1, L0_ffn_W2, L0_ffn_b2):
    import jax
    import jax.numpy as jnp

    def _L0_conv_ref(x, W_prep, b_prep, intrinsic, W_fin, b_fin):
        import jax, jax.numpy as jnp
        import numpy as np
        B, HIMG, WIMG, C = (2, 32, 32, 64)
        NH, HD = (8, 32)
        WH, WW = (8, 8)
        P = WH * WW
        NQK = 5
        S = 1 + HD + HD
        EPS = 1e-05

        def _spatial(intrinsic):
            ii = jnp.arange(WH)
            jj = jnp.arange(WW)
            ri = ii[:, None] - ii[None, :] + WH - 1
            rj = jj[:, None] - jj[None, :] + WW - 1
            rel = intrinsic[:, ri[:, None, :, None], rj[None, :, None, :], :]
            rel = rel.transpose(1, 2, 0, 3, 4, 5).reshape(P, NH, P, S)
            return (rel[..., 0], rel[..., 1:1 + HD], rel[..., 1 + HD:])
        t = x @ W_prep + b_prep
        nwh, nww = (HIMG // WH, WIMG // WW)
        wins = t.reshape(B, nwh, WH, nww, WW, NQK, NH, HD).transpose(0, 1, 3, 2, 4, 5, 6, 7)
        wins = wins.reshape(B * nwh * nww, P, NQK, NH, HD)
        wins = wins.transpose(2, 0, 3, 1, 4)
        q_n, q, k, k_m, v = (wins[i] for i in range(NQK))
        bias, pat_n, pat_m = _spatial(intrinsic)
        score = bias[None]
        score = score + jnp.einsum('bhod,ohid->bohi', q_n, pat_n)
        score = score + jnp.einsum('bhod,bhid->bohi', q, k)
        score = score + jnp.einsum('bhid,ohid->bohi', k_m, pat_m)
        mean = jnp.mean(score, axis=-1, keepdims=True)
        std = jnp.sqrt(jnp.var(score, axis=-1, ddof=1, keepdims=True) + EPS)
        score = (score - mean) / std
        out = jnp.einsum('bohi,bhid->bohd', score, v)
        out = out.reshape(B, nwh, nww, WH, WW, NH * HD).transpose(0, 1, 3, 2, 4, 5)
        out = out.reshape(B, HIMG, WIMG, NH * HD)
        return out @ W_fin + b_fin

    def _L0_ffn_ref(x, Wr, br, ln_g, ln_b, W1, b1, W2, b2):
        import jax, jax.numpy as jnp
        import numpy as np
        TOP_K = 2
        LN_EPS = 1e-05
        B, S, D = x.shape
        N = B * S
        xt = x.reshape(N, D)
        logits = xt @ Wr + br
        probs = jax.nn.softmax(logits, axis=-1)
        top_p, top_idx = jax.lax.top_k(probs, TOP_K)
        weights = top_p / top_p.sum(axis=-1, keepdims=True)
        mu = xt.mean(axis=-1, keepdims=True)
        var = ((xt - mu) ** 2).mean(axis=-1, keepdims=True)
        xn = (xt - mu) * jax.lax.rsqrt(var + LN_EPS)
        xe = xn[None, :, :] * ln_g[:, None, :] + ln_b[:, None, :]
        h = jax.nn.gelu(jnp.einsum('end,edh->enh', xe, W1) + b1[:, None, :], approximate=False)
        y = jnp.einsum('enh,ehd->end', h, W2) + b2[:, None, :]
        y_tok = jnp.transpose(y, (1, 0, 2))
        sel = jnp.take_along_axis(y_tok, top_idx[:, :, None], axis=1)
        out = (weights[:, :, None] * sel).sum(axis=1)
        return out.reshape(B, S, D)

    def _gn(v, G=32, eps=1e-05):
        B_, H_, W_, C_ = v.shape
        g = v.reshape(B_, H_, W_, G, C_ // G)
        m = jnp.mean(g, axis=(1, 2, 4), keepdims=True)
        s = jnp.var(g, axis=(1, 2, 4), keepdims=True)
        return ((g - m) / jnp.sqrt(s + eps)).reshape(v.shape)

    def _ln_c(v, eps=1e-06):
        m = jnp.mean(v, axis=-1, keepdims=True)
        s = jnp.var(v, axis=-1, keepdims=True)
        return (v - m) / jnp.sqrt(s + eps)

    def _ln_t(v, eps=1e-05):
        m = jnp.mean(v, axis=-1, keepdims=True)
        s = jnp.var(v, axis=-1, keepdims=True)
        return (v - m) / jnp.sqrt(s + eps)

    def _to_tokens(v):
        B_, H_, W_, C_ = v.shape
        return v.reshape(B_, H_ * W_, C_)

    def _from_tokens(t, like):
        return t.reshape(like.shape)
    x = x + _L0_conv_ref(_ln_c(x), L0_conv_W_prep, L0_conv_b_prep, L0_conv_intrinsic, L0_conv_W_fin, L0_conv_b_fin)
    t = _to_tokens(x)
    t = t + _L0_ffn_ref(_ln_t(t), L0_ffn_Wr, L0_ffn_br, L0_ffn_ln_g, L0_ffn_ln_b, L0_ffn_W1, L0_ffn_b1, L0_ffn_W2, L0_ffn_b2)
    x = _from_tokens(t, x)
    return x

_drawn_inputs = setup_inputs


def setup_inputs(seed=0):
    import zlib

    import numpy as np

    out = dict(_drawn_inputs(seed))
    spreads = {'L0_conv_b_prep': (0.0, 0.1),
     'L0_conv_b_fin': (0.0, 0.767),
     'L0_ffn_br': (0.0, 0.432),
     'L0_ffn_ln_g': (1.0, 0.6),
     'L0_ffn_ln_b': (0.0, 0.8),
     'L0_ffn_b1': (0.0, 0.8),
     'L0_ffn_b2': (0.0, 0.8)}
    factors = {}
    for name, (base, spread) in spreads.items():
        noise = np.random.default_rng([zlib.crc32(name.encode()), seed]).standard_normal(out[name].shape)
        drawn = base * np.exp(spread * noise) if base else spread * noise
        out[name] = jnp.asarray(drawn.astype(out[name].dtype))
    for name, factor in factors.items():
        out[name] = (out[name] * factor).astype(out[name].dtype)
    return out
```

```python
from contextlib import ExitStack

import concourse.bass as bass
from concourse import mybir

F32 = mybir.dt.float32
F32R = mybir.dt.float32r
BF16 = mybir.dt.bfloat16
ALU = mybir.AluOpType
ACT = mybir.ActivationFunctionType
AX = mybir.AxisListType

P = 128
C = 64
NH, HD = 8, 32
WH = 8
WT = WH * WH
NW = 32
NPAIR = NW // 2
NG = NPAIR // 4
TOK = NW * WT
SIDE = 2 * WH - 1
NREL = SIDE * SIDE
NE, HID = 8, 256
EPS_C, EPS_T, EPS_S = 1e-6, 1e-5, 1e-5
QN, Q, K_, KM, V = range(5)
KINDS = [QN, QN, KM, KM, Q, Q]


def make_plan():
    plan = [(("b1",), 7, 1)]
    for j in range(NG):
        plan += [(("xt", j), j, 1), (("xc", j), 4 + j, 1)]
    for s in range(NG):
        plan += [(("k", g, s), (2 * s + g) % 4, 1) for g in range(2)]

    def prep(c, n):
        return [(("bd", c, n), 4 + n % 2, 2)]

    for c in range(2):
        for n in range(4):
            plan += prep(c, n)
    for c in range(4):
        for i in range(8):
            plan += [(("t", 8 * c + i), i % 4, 1)]
            if c >= 1 and i % 2 == 0:
                plan += prep(c + 1, i // 2)
    for step in range(18 + NG * 4 + 4):
        plan += [(u, b, r) for u, b, r in pe_steps(step)]
    return plan


def pe_steps(t):
    s = []
    if t < NPAIR:
        if t == 0:
            s.append((("v", 0), 6, 1))
        s.append((("score", t), t % 2, 1))
        if t + 1 < NPAIR:
            s.append((("v", t + 1), 6, 1))
        if t == 0:
            s += [(("bd", 5, n), (5, 7, 4, 3)[n], 2) for n in range(4)]
    if 1 <= t <= NPAIR:
        s.append((("o", t - 1), 2 + (t - 1) % 2, 1))
    if 2 <= t <= NPAIR + 1 and (t - 2) % 4 == 3:
        s.append((("ss", (t - 2) // 4), 4, 1))
    elif 2 <= t <= NPAIR + 1:
        s.append((("ss part", t - 2), 4, 0))
    j, r = divmod(t - 6, 4)
    if r == 0 and 0 <= j < NG:
        s.append((("st", j), 5, 1))
    j, r = divmod(t - 9, 4)
    if r == 0 and 0 <= j < NG:
        s += [(("on", j, 0), 5, 1), (("on", j, 1), 5, 1), (("y", j), 7, 1)]
    j, r = divmod(t - 11, 4)
    if r == 0 and 0 <= j < NG:
        s.append((("zt", j), 6, 1))
    j, r = divmod(t - 12, 4)
    if r == 0 and 0 <= j < NG:
        s += [(("lg", j), 6, 1), (("x2", j), 7, 1)]
    j, r = divmod(t - 13, 4)
    if r == 0 and 0 <= j < NG:
        s.append((("gt", j), 7, 1))
    u = t - 18
    if 0 <= u < 4 * NG:
        s.append((("gb", u), 5, 1))
        s += [(("h", 4 * u), (4 * u) % 3, 1), (("h", 4 * u + 1), (4 * u + 1) % 3, 1)]
    if 1 <= u <= 4 * NG:
        s.append((("e", u - 1), 3 + (u - 1) % 2, 1))
    if 0 <= u < 4 * NG:
        s += [(("h", 4 * u + 2), (4 * u + 2) % 3, 1), (("h", 4 * u + 3), (4 * u + 3) % 3, 1)]
        s.append((("e part", u), 3 + u % 2, 0))
    j, r = divmod(t - 23, 4)
    if r == 0 and 0 <= j < NG:
        s.append((("out", j), 6, 1))
    return s


def metaformer_kernel(nc, x, W_prep, b_prep, rel, rel0, W_fin, b_fin, Wr, br, ln_g, ln_b, W1, b1,
                      W2, b2, out):
    before, at_fill, at_drain = {}, {}, {}
    fills, drains = [0] * 8, [0] * 8
    open_part = {}
    for use, bank, readers in make_plan():
        if readers == 0:
            if bank not in open_part:
                open_part[bank] = drains[bank]
            before[use] = (bank, open_part[bank])
            continue
        before[use] = (bank, open_part.pop(bank, drains[bank]))
        fills[bank] += 1
        drains[bank] += readers
        at_fill[use], at_drain[use] = (bank, fills[bank]), (bank, drains[bank])

    with ExitStack() as ctx:
        sem = lambda name: ctx.enter_context(nc.semaphore(name))
        bank_filled = [sem(f"bank{b}_filled") for b in range(8)]
        bank_drained = [sem(f"bank{b}_drained") for b in range(8)]
        PS = [ctx.enter_context(nc.psum_tensor(f"PS{b}", [P, 512], F32)) for b in range(8)]

        def filled(*use):
            return bank_filled[at_fill[use][0]], at_fill[use][1]

        def drained(*use):
            return bank_drained[at_drain[use][0]], at_drain[use][1]

        base = 16640
        arena = ctx.enter_context(nc.sbuf_tensor("arena", [P, (229344 - base - 512) // 4], F32))
        cursor = [base]

        def sb(name, shape, dt=F32, at=None):
            size = 2 if dt == BF16 else 4
            for n in shape[1:]:
                size *= n
            size = -(-size // 32) * 32
            where = at if at is not None else cursor
            t = nc.alloc_sbuf_tensor_at(name, shape, dt, offset=where[0])
            where[0] += size
            return t

        XR = sb("XR", [P, NPAIR, C])
        W2s = sb("W2s", [P, 16, C])
        KT = sb("KT", [P, 2, TOK])
        XC = sb("XC", [C, TOK])
        WV = sb("WV", [C, 256])
        WF = sb("WF", [P, 2, C])
        IDN = sb("IDN", [P, P])
        IDB = sb("IDB", [P, P], BF16)
        CEN = sb("CEN", [P, P])
        II = sb("II", [P, C])
        ONES2 = sb("ONES2", [P, 32])
        SEL = sb("SEL", [24, 4, P], BF16)
        TRI = sb("TRI", [P, NE, NE])
        NHALF = sb("NHALF", [P, 32])
        BP = sb("BP", [P, 10])
        B1 = sb("B1", [P, 16])
        B1P = sb("B1P", [P, 16])
        B2 = sb("B2", [P, 4])
        LNG = sb("LNG", [P, NE])
        LNB = sb("LNB", [C, NE])
        BRB = sb("BRB", [P, NE])
        WRs = sb("WRs", [C, NE])
        S1 = sb("S1", [P, NG, 4])
        S2 = sb("S2", [P, NG, 4])
        RS = sb("RS", [P, NG, 4])
        tn_at = [cursor[0]]
        TN = sb("TN", [P, NPAIR, 4, 2, WT])
        tm_at = [cursor[0]]
        TM = sb("TM", [P, P, WT])
        bd_at = [[cursor[0]], [cursor[0] + 32768]]
        BD = [sb(f"BD{n}", [P, 2, 4, 1024]) for n in range(2)]
        region = cursor[0]

        XN = sb("XN", [P, NPAIR, 2, C], at=tm_at)
        XM = sb("XM", [P, NPAIR, C], at=tm_at)
        WS = sb("WS", [P, 1280], at=tm_at)
        REL = sb("REL", [P, 2, 2, NREL], at=tm_at)
        PN = sb("PN", [P, 2, WH, SIDE, WH], at=tm_at)
        W1E = sb("W1E", [C, NE * HID], at=tn_at)
        BFB = sb("BFB", [P, C], at=tn_at)
        r_at = [region]
        WHI = sb("WHI", [P, 1280], F32R, at=r_at)
        WLO = sb("WLO", [P, 1280], F32R, at=r_at)
        XS = sb("XS", [P, NW, WT], F32R, at=r_at)
        ab_at = [r_at[0]]
        PM = sb("PM", [P, 2, WH, SIDE, WH], at=r_at)
        BI = sb("BI", [P, 4, WT], at=r_at)
        RB = sb("RB", [NH, NREL], at=r_at)
        EB = sb("EB", [NH, WH, SIDE, WH], at=r_at)
        SR = [sb(f"SR{n}", [P, 512], at=ab_at) for n in range(3)]
        SQ = [sb(f"SQ{n}", [P, 512], at=ab_at) for n in range(2)]
        BV = [sb(f"BV{n}", [P, NH, 2, HD + 1], at=ab_at) for n in range(3)]
        late = [region]
        OR = sb("OR", [P, 8, 4, 2, HD + 1], at=late)
        ON = sb("ON", [P, 4, 2, 4, HD], at=late)
        ONT = sb("ONT", [P, 4, 2, P], at=late)
        VA = sb("VA", [P, 4, 4, 2], at=late)
        VB = sb("VB", [P, 4, 4, 2], at=late)
        RSC = sb("RSC", [P, 4, 4, 2], at=late)
        PX = sb("PX", [P, 4, NE], at=late)
        M1 = sb("M1", [P, 4], at=late)
        M2 = sb("M2", [P, 4], at=late)
        G3 = sb("G3", [P, 4, 3, NE], BF16, at=late)
        sqx_at = [late[0]]
        SQX = sb("SQX", [P, 4, C], at=late)
        CG = sb("CG", [P, 4, NE, NE], at=sqx_at)
        assert late[0] <= region + 5120 * 2 + 8192, (late, region)
        rest = [max(ab_at[0], r_at[0])]
        SSB = sb("SSB", [P, 512], at=rest)
        ZT = sb("ZT", [C, 512], at=rest)
        LG = sb("LG", [P, 4, NE], at=rest)
        PR = sb("PR", [P, 4, NE], at=rest)
        Z = sb("Z", [P, 4, C], at=rest)
        Z2 = sb("Z2", [P, 4, 2, C], at=rest)
        xms_at = [rest[0]]
        XMS = sb("XMS", [P, 4, C], at=rest)
        CE = sb("CE", [P, 4, NE, NE], at=xms_at)
        assert rest[0] <= 229344, rest
        W1H = sb("W1H", [P, NE * HID], F32R, at=bd_at[0])
        W1L = sb("W1L", [P, NE * HID], F32R, at=bd_at[0])
        X2 = sb("X2", [P, TOK], F32R, at=bd_at[0])
        W1R = sb("W1R", [P, 4, HID], at=bd_at[0])
        GT = sb("GT", [24, TOK], BF16, at=bd_at[0])
        HR = [sb(f"HR{n}", [P, 512], at=bd_at[1]) for n in range(4)]
        GB = [sb(f"GB{n}", [P, 512], at=bd_at[1]) for n in range(2)]
        AC = [sb(f"AC{n}", [P, 512], at=bd_at[1]) for n in range(2)]
        GM = sb("GM", [P, 512], at=bd_at[1])
        scratch = nc.dram_tensor("bias_rows", [NH, WH, SIDE * WH], F32).ap()

        x_in = [sem(f"x_in{j}") for j in range(NG)]
        wprep_in = sem("wprep_in")
        w1e_in = sem("w1e_in")
        lnb_in = sem("lnb_in")
        rel_in = sem("rel_in")
        rel0_in = sem("rel0_in")
        small_in = sem("small_in")
        bias_out = sem("bias_out")
        bias_in = sem("bias_in")
        w1r_in = sem("w1r_in")
        result_out = sem("result_out")
        dve_step = sem("dve_step")
        act_step = sem("act_step")
        pool_step = sem("pool_step")
        consts_ready = sem("consts_ready")
        bd_zeroed = sem("bd_zeroed")
        bv_zeroed = sem("bv_zeroed")
        pm_ready = sem("pm_ready")
        pn_ready = sem("pn_ready")
        bias_rows = sem("bias_rows_ready")
        whi_ready = sem("whi_ready")
        wlo_ready = sem("wlo_ready")
        var_ready = sem("var_ready")
        rstd_ready = sem("rstd_ready")
        xn_ready = sem("xn_ready")
        xhi_ready = sem("xhi_ready")
        sq_ready = sem("sq_ready")
        on_ready = sem("on_ready")
        z_ready = sem("z_ready")
        z2_ready = sem("z2_ready")
        x2hi_ready = sem("x2hi_ready")
        lg_ready = sem("lg_ready")
        px_ready = sem("px_ready")
        g3_ready = sem("g3_ready")
        w1h_ready = sem("w1h_ready")
        w1l_ready = sem("w1l_ready")
        down_done = sem("down_done")
        gate_done = sem("gate_done")
        sq_used = sem("sq_used")
        b1p_ready = sem("b1p_ready")

        asks = [("x", j) for j in range(NG)]
        for t in range(NPAIR + 24):
            for kind, off in (("o", 6), ("z", 9), ("z2", 10)):
                j, r = divmod(t - off, 4)
                if r == 0 and 0 <= j < NG:
                    asks.append((kind, j))
        ask_no = {a: n + 1 for n, a in enumerate(asks)}

        block = ctx.enter_context(nc.Block())

        @block.sync
        def _(sp):
            for j in range(NG):
                sp.dma_start(XR[:, 4 * j:4 * j + 4, :], x[:, 4 * j:4 * j + 4, :]).then_inc(x_in[j], 16)
            sp.dma_start(WS[0:C, :], W_prep).then_inc(wprep_in, 16)
            sp.dma_start(WS[C:P, :], W_prep).then_inc(wprep_in, 16)
            sp.dma_start(W1E[:, :].rearrange("p (e h) -> p e h", e=NE), W1).then_inc(w1e_in, 16)
            sp.dma_start(REL[:, :, :, :], rel).then_inc(rel_in, 16)
            for dst, src in ((BP[:, :], b_prep), (WV[:, :], W_prep[:, V * 256:]), (B1[:, :], b1),
                             (B2[:, :], b2), (LNG[0:C, :], ln_g), (LNG[C:P, :], ln_g),
                             (BFB[:, :], b_fin.partition_broadcast(P)),
                             (BRB[:, :], br.partition_broadcast(P)), (WRs[:, :], Wr),
                             (WF[:, :, :], W_fin), (W2s[:, :, :], W2)):
                sp.dma_start(dst, src).then_inc(small_in, 16)
            sp.wait_ge(bias_rows, 1)
            sp.dma_start(scratch, EB[:, :, :, :].rearrange("h j r c -> h j (r c)")).then_inc(bias_out, 16)
            sp.wait_ge(bias_out, 16)
            for g in range(2):
                for ii in range(WH):
                    lo = (WH - 1 - ii) * WH
                    src = scratch[4 * g:4 * g + 4, :, lo:lo + WT].rearrange("h j o -> j h o")
                    r0 = g * C + ii * WH
                    sp.dma_start(BI[r0:r0 + WH, :, :], src).then_inc(bias_in, 16)
            sp.wait_ge(*filled("score", NPAIR // 2 - 1))
            for half in range(2):
                if half:
                    sp.wait_ge(w1l_ready, 4)
                for d in range(2):
                    sp.dma_start(W1R[d * C:d * C + C, :, :], W1[:, 4 * half:4 * half + 4, :]).then_inc(w1r_in, 16)
            for j in range(NG):
                sp.wait_ge(*drained("out", j))
                sp.dma_start(out[:, 4 * j:4 * j + 4, :], XR[:, 4 * j:4 * j + 4, :]).then_inc(result_out, 16)
            sp.wait_ge(result_out, 16 * NG)

        N_SMALL = 11

        @block.gpsimd
        def _(pool):
            n = [0]

            def step(ins):
                n[0] += 1
                ins.then_inc(pool_step, 1)
                pool.wait_ge(pool_step, n[0])

            pool.dma_start(LNB[:, :], ln_b).then_inc(lnb_in, 16)
            pool.dma_start(RB[:, :], rel0).then_inc(rel0_in, 16)
            step(pool.memset(IDN[:, :], 0.0))
            pool.affine_select(out=IDN[:, :], in_=IDN[:, :], compare_op=ALU.not_equal, fill=1.0, base=0,
                               pattern=[[-1, P]], channel_multiplier=1).then_inc(consts_ready, 1)
            step(pool.memset(NHALF[:, :], -0.5))
            step(pool.memset(CEN[:, :], 0.0))
            step(pool.memset(CEN[0:C, 0:C], -1.0 / WT))
            step(pool.memset(CEN[C:P, C:P], -1.0 / WT))
            pool.wait_ge(consts_ready, 1)
            pool.tensor_tensor(CEN[:, :], CEN[:, :], IDN[:, :], ALU.add).then_inc(consts_ready, 1)

            def power(kind, j):
                pool.wait_ge(var_ready, ask_no[(kind, j)])
                if kind == "o":
                    pool.tensor_tensor(RSC[:, :, :, :].rearrange("p a b c -> p (a b c)"),
                                       VB[:, :, :, :].rearrange("p a b c -> p (a b c)"),
                                       NHALF[:, :], ALU.pow).then_inc(rstd_ready, 1)
                else:
                    pool.tensor_tensor(RS[:, j, :], S2[:, j, :], NHALF[:, 0:4], ALU.pow).then_inc(rstd_ready, 1)

            power("x", 0)
            power("x", 1)
            power("x", 2)
            power("x", 3)
            pool.memset(BD[0][:, :, :, :], 0.0).then_inc(bd_zeroed, 1)
            pool.memset(BD[1][:, :, :, :], 0.0).then_inc(bd_zeroed, 1)
            pool.wait_ge(rel_in, 16)
            for ij in range(WH):
                src = REL[:, 1, :, :].rearrange("p g (r c) -> p g r c", c=SIDE)
                pool.tensor_copy(PM[:, :, ij, :, :], src[:, :, :, WH - 1 - ij:2 * WH - 1 - ij]).then_inc(pm_ready, 1)
            step(pool.memset(ONES2[:, :], 0.0))
            step(pool.memset(ONES2[0:C, 0:1], 1.0))
            step(pool.memset(ONES2[C:P, 1:2], 1.0))
            step(pool.memset(II[:, :], 0.0))
            for d in range(2):
                step(pool.affine_select(out=II[:, :], in_=II[:, :], compare_op=ALU.not_equal, fill=1.0,
                                        base=-C * d, pattern=[[-1, C]], channel_multiplier=1))
            step(pool.memset(SEL[:, :, :], 0.0))
            sel = SEL[:, :, :].rearrange("k p (d c) -> k p d c", d=2)
            for part in range(3):
                step(pool.affine_select(out=sel, in_=sel, compare_op=ALU.not_equal, fill=1.0, base=-NE * part,
                                        pattern=[[-2, 4], [-1, 2], [0, C]], channel_multiplier=1))
            step(pool.memset(TRI[:, :, :], 1.0))
            step(pool.affine_select(out=TRI[:, :, :], in_=TRI[:, :, :], compare_op=ALU.is_gt, fill=0.0, base=0,
                                    pattern=[[1, NE], [-1, NE]], channel_multiplier=0))
            pool.tensor_copy(IDB[:, :], IDN[:, :]).then_inc(consts_ready, 1)
            pool.wait_ge(*filled("t", 31))
            for v in BV:
                step(pool.memset(v[:, :, :, :], 0.0))
            for v in BV:
                step(pool.memset(v[0:C, :, 0, HD:HD + 1], 1.0))
                pool.memset(v[C:P, :, 1, HD:HD + 1], 1.0).then_inc(bv_zeroed, 1)
            for kind, j in asks[NG:]:
                power(kind, j)

        @block.tensor
        def _(pe):
            def begin(*use):
                bank, count = before[use]
                if count:
                    pe.wait_ge(bank_drained[bank], count)
                return PS[bank]

            def end(ins, *use):
                ins.then_inc(bank_filled[at_fill[use][0]], 1)

            pe.wait_ge(w1e_in, 16)
            pe.wait_ge(lnb_in, 16)
            ps = begin("b1")
            for e in range(NE):
                for c in range(2):
                    m = nc.tensor.matmul(ps[:, 2 * e + c:2 * e + c + 1], W1E[:, e * HID + c * P:e * HID + c * P + P],
                                         LNB[:, e:e + 1], start=True, stop=True)
            end(m, "b1")

            pe.wait_ge(consts_ready, 2)
            for j in range(NG):
                pe.wait_ge(xn_ready, j + 1)
                ps = begin("xt", j)
                for n in range(4):
                    m = nc.tensor.transpose(ps[:, n * P:n * P + P],
                                            XN[:, 4 * j + n, :, :].rearrange("p d c -> p (d c)"), IDN[:, :])
                end(m, "xt", j)
                ps = begin("xc", j)
                for n in range(4):
                    m = nc.tensor.matmul(ps[0:C, n * P:n * P + P], XN[:, 4 * j + n, 0, :], CEN[:, :],
                                         start=True, stop=True)
                end(m, "xc", j)

            def project(ps, kind, g, moving):
                col = kind * 256 + g * P
                nc.tensor.matmul(ps[:, :], WHI[:, col:col + P], moving, start=True, stop=False)
                return nc.tensor.matmul(ps[:, :], WLO[:, col:col + P], moving, start=False, stop=True)

            pe.wait_ge(whi_ready, 1)
            pe.wait_ge(wlo_ready, 1)
            for s in range(NG):
                pe.wait_ge(*drained("xt", s))
                for g in range(2):
                    ps = begin("k", g, s)
                    end(project(ps, K_, g, XS[:, 8 * s:8 * s + 8, :]), "k", g, s)

            def prep(c, n):
                g, s = divmod(n, 2)
                half = c % 2
                if KINDS[c] == Q:
                    w0 = 16 * half + 8 * s
                    moving = XS[:, w0:w0 + 8, :]
                else:
                    moving = XS[:, 16 * s:16 * s + 16, 32 * half:32 * half + 32]
                ps = begin("bd", c, n)
                end(project(ps, KINDS[c], g, moving), "bd", c, n)

            def pattern(tile):
                c, i = divmod(tile, 8)
                table = PN if c < 2 else PM
                slot = BD[c % 2]
                if i == 0:
                    pe.wait_ge(*drained("bd", c, 3))
                    pe.wait_ge(*drained("bd", c, 2))
                ps = begin("t", tile)
                for u in range(4):
                    local = 4 * i + u
                    fy, fx = divmod(32 * (c % 2) + local, WH)
                    for g in range(2):
                        rows = table[:, g, fx, WH - 1 - fy:2 * WH - 1 - fy, :].rearrange("p a b -> p (a b)")
                        moving = slot[:, g, :, 32 * local:32 * local + 32]
                        m = nc.tensor.matmul(ps[g * C:g * C + C, u * P:u * P + P], rows, moving,
                                             start=True, stop=True)
                end(m, "t", tile)

            for c in range(2):
                for n in range(4):
                    prep(c, n)
            pe.wait_ge(pn_ready, 1)
            for c in range(4):
                if c == 2:
                    pe.wait_ge(pm_ready, WH)
                for i in range(8):
                    pattern(8 * c + i)
                    if c >= 1 and i % 2 == 0:
                        prep(c + 1, i // 2)

            def values(t):
                ps = begin("v", t)
                end(nc.tensor.matmul(ps[:, 0:256], XC[:, t * P:t * P + P], WV[:, :], start=True, stop=True), "v", t)

            def score(t):
                if t == 0:
                    pe.wait_ge(*drained("t", 31))
                    pe.wait_ge(*drained("bd", 4, 2))
                    pe.wait_ge(*drained("bd", 4, 3))
                if t == NPAIR // 2:
                    for n in range(4):
                        pe.wait_ge(*drained("bd", 5, n))
                slot = BD[t // (NPAIR // 2)]
                ps = begin("score", t)
                for h in range(4):
                    pair = TM[:, h * NW + 2 * t:h * NW + 2 * t + 2, :].rearrange("p w i -> p (w i)")
                    nc.tensor.matmul(ps[:, h * P:h * P + P], pair, IDN[:, :], start=(h == 0), stop=False,
                                     skip_group_check=True)
                for g in range(2):
                    for w in range(2):
                        lo = (2 * t + w) * WT
                        lq = lo % 1024
                        dst = ps[w * C:w * C + C, :].rearrange("p (h g o) -> p h g o", h=4, g=2)[:, :, g, :]
                        m = nc.tensor.matmul(dst, KT[:, g, lo:lo + WT], slot[:, g, :, lq:lq + WT],
                                             start=False, stop=True, skip_group_check=True)
                end(m, "score", t)

            def weighted(t):
                pe.wait_ge(*drained("score", t))
                pe.wait_ge(*drained("v", t))
                ps = begin("o", t)
                for h in range(4):
                    for g in range(2):
                        dst = ps[g * C:g * C + C, h * 66:h * 66 + 66]
                        m = nc.tensor.matmul(dst, SR[t % 3][:, (2 * h + g) * C:(2 * h + g) * C + C],
                                             BV[t % 3][:, 4 * g + h, :, :].rearrange("p w d -> p (w d)"),
                                             start=True, stop=True)
                end(m, "o", t)

            def squares(t):
                q = t % 4
                pe.wait_ge(sq_ready, t + 1)
                last = q == 3
                ps = begin("ss", t // 4) if last else begin("ss part", t)
                m = nc.tensor.matmul(ps[32 * q:32 * q + 32, :], ONES2[:, :], SQ[t % 2][:, :], start=True, stop=True)
                m.then_inc(bank_filled[4] if last else sq_used, 1)

            def hidden(n):
                u, r = divmod(n, 4)
                j, ep = divmod(u, 4)
                c, d = divmod(r, 2)
                col = (2 * ep + d) * HID + c * P
                ps = begin("h", n)
                nc.tensor.matmul(ps[:, :], W1H[:, col:col + P], X2[:, j * 512:j * 512 + 512], start=True, stop=False)
                end(nc.tensor.matmul(ps[:, :], W1L[:, col:col + P], X2[:, j * 512:j * 512 + 512],
                                     start=False, stop=True), "h", n)

            def down(u, c):
                ep = u % 4
                pe.wait_ge(*drained("h", 4 * u + 2 * c))
                pe.wait_ge(*drained("h", 4 * u + 2 * c + 1))
                ps = begin("e part", u) if c == 0 else PS[before[("e", u)][0]]
                for d in range(2):
                    m = nc.tensor.matmul(ps[d * C:d * C + C, :], W2s[:, 2 * (2 * ep + d) + c, :],
                                         HR[(2 * c + d) % 4][:, :], start=(c == 0), stop=(c == 1),
                                         skip_group_check=True)
                m.then_inc(down_done if c == 0 else bank_filled[before[("e", u)][0]], 1)

            for t in range(18 + 4 * NG + 4):
                for use, _, _ in pe_steps(t):
                    kind, a = use[0], use[1]
                    if kind == "v":
                        if a == 0:
                            pe.wait_ge(small_in, 16 * N_SMALL)
                            pe.wait_ge(*drained("xc", NG - 1))
                        values(a)
                    elif kind == "score":
                        score(a)
                    elif kind == "bd":
                        prep(5, use[2])
                    elif kind == "o":
                        if a == 0:
                            pe.wait_ge(bv_zeroed, 3)
                        weighted(a)
                    elif kind == "ss part":
                        if a == 0:
                            pe.wait_ge(consts_ready, 3)
                        squares(a)
                    elif kind == "ss":
                        squares(4 * a + 3)
                    elif kind == "st":
                        pe.wait_ge(*drained("ss", a))
                        ps = begin("st", a)
                        for h in range(4):
                            m = nc.tensor.transpose(ps[:, h * P:h * P + P], SSB[:, h * P:h * P + P], IDN[:, :])
                        end(m, "st", a)
                    elif kind == "on":
                        half = use[2]
                        pe.wait_ge(on_ready, 4 * a + 2 * half + 2)
                        ps = begin("on", a, half)
                        for q in range(2):
                            for w in range(2):
                                m = nc.tensor.transpose(ps[:, (2 * q + w) * P:(2 * q + w) * P + P],
                                                        ON[:, 2 * half + q, w, :, :].rearrange("p h d -> p (h d)"),
                                                        IDN[:, :])
                        end(m, "on", a, half)
                    elif kind == "y":
                        pe.wait_ge(*drained("on", a, 1))
                        ps = begin("y", a)
                        for q in range(4):
                            for g in range(2):
                                m = nc.tensor.matmul(ps[:, q * C:q * C + C], ONT[:, q, g, :], WF[:, g, :],
                                                     start=(g == 0), stop=(g == 1))
                        end(m, "y", a)
                    elif kind == "zt":
                        pe.wait_ge(z_ready, a + 1)
                        ps = begin("zt", a)
                        for q in range(4):
                            m = nc.tensor.transpose(ps[0:C, q * P:q * P + P], Z[:, q, :], IDN[:, :])
                        end(m, "zt", a)
                    elif kind == "lg":
                        pe.wait_ge(*drained("zt", a))
                        ps = begin("lg", a)
                        for q in range(4):
                            m = nc.tensor.matmul(ps[:, q * NE:q * NE + NE], ZT[:, q * P:q * P + P], WRs[:, :],
                                                 start=True, stop=True)
                        end(m, "lg", a)
                    elif kind == "x2":
                        pe.wait_ge(z2_ready, a + 1)
                        ps = begin("x2", a)
                        for q in range(4):
                            m = nc.tensor.transpose(ps[:, q * P:q * P + P],
                                                    Z2[:, q, :, :].rearrange("p d c -> p (d c)"), IDN[:, :])
                        end(m, "x2", a)
                    elif kind == "gt":
                        pe.wait_ge(g3_ready, a + 1)
                        ps = begin("gt", a)
                        half_words = ps[0:24, 0:256].bitcast(BF16)
                        for q in range(4):
                            m = nc.tensor.transpose(half_words[:, q * P:q * P + P],
                                                    G3[:, q, :, :].rearrange("p k e -> p (k e)"), IDB[:, :])
                        end(m, "gt", a)
                    elif kind == "gb":
                        if a % 4 == 0:
                            pe.wait_ge(*drained("gt", a // 4))
                        ps = begin("gb", a)
                        end(nc.tensor.matmul(ps[:, :], SEL[:, a % 4, :], GT[:, (a // 4) * 512:(a // 4) * 512 + 512],
                                             start=True, stop=True), "gb", a)
                    elif kind == "h":
                        if a == 0:
                            pe.wait_ge(w1h_ready, NE)
                            pe.wait_ge(w1l_ready, NE)
                        if a % 16 == 0:
                            pe.wait_ge(*drained("x2", a // 16))
                        hidden(a)
                    elif kind == "e part":
                        down(a, 0)
                    elif kind == "e":
                        down(a, 1)
                    elif kind == "out":
                        pe.wait_ge(gate_done, 3 * a + 3)
                        ps = begin("out", a)
                        for q in range(4):
                            m = nc.tensor.matmul(ps[:, q * C:q * C + C], AC[a % 2][:, q * P:q * P + P], II[:, :],
                                                 start=True, stop=True)
                        end(m, "out", a)

        @block.scalar
        def _(act):
            A = nc.scalar.activation
            act.wait_ge(wprep_in, 32)
            A(WHI[:, :], WS[:, :], ACT.Copy).then_inc(whi_ready, 1)
            for j in range(NG):
                act.wait_ge(*filled("xt", j))
                A(XS[:, 8 * j:8 * j + 8, :].rearrange("p w o -> p (w o)"), PS[j][:, :],
                  ACT.Copy).then_inc(xhi_ready, 1)
                act.wait_ge(*filled("xc", j))
                A(XC[:, 512 * j:512 * j + 512], PS[4 + j][0:C, :], ACT.Copy).then_inc(bank_drained[4 + j], 1)
            act.wait_ge(small_in, 16 * N_SMALL)
            for s in range(NG):
                for g in range(2):
                    act.wait_ge(*filled("k", g, s))
                    b = (2 * s + g) % 4
                    A(KT[:, g, 512 * s:512 * s + 512], PS[b][:, :], ACT.Identity,
                      bias=BP[:, 2 * K_ + g:2 * K_ + g + 1]).then_inc(bank_drained[b], 1)

            def spread(c, n, heads):
                g, s = divmod(n, 2)
                b = before[("bd", c, n)][0]
                if n == 0:
                    act.wait_ge(bd_zeroed, c % 2 + 1)
                    if c >= 2:
                        act.wait_ge(*filled("t", 8 * (c - 2) + 7))
                act.wait_ge(*filled("bd", c, n))
                for h in heads:
                    r = slice(HD * h, HD * h + HD)
                    bias = BP[r, 2 * KINDS[c] + g:2 * KINDS[c] + g + 1]
                    dst = BD[c % 2][r, g, h, :]
                    if KINDS[c] == Q:
                        last = A(dst[:, 512 * s:512 * s + 512], PS[b][r, :], ACT.Identity, bias=bias)
                    else:
                        dst = dst.rearrange("p (o w) -> p w o", w=NW)[:, 16 * s:16 * s + 16, :]
                        last = A(dst, PS[b][r, :].rearrange("p (w o) -> p w o", w=16), ACT.Identity, bias=bias)
                last.then_inc(bank_drained[b], 1)

            for c in range(2):
                for n in range(4):
                    spread(c, n, range(2))
            for c in range(4):
                for i in range(8):
                    tile = 8 * c + i
                    if c >= 2:
                        act.wait_ge(*filled("t", tile))
                        i0 = 4 * (tile - 16)
                        A(TM[:, :, i0:i0 + 4].rearrange("p w i -> p i w"),
                          PS[tile % 4][:, :].rearrange("p (i w) -> p i w", i=4), ACT.Copy)\
                            .then_inc(bank_drained[tile % 4], 1)
                    if c >= 1 and i % 2 == 0:
                        spread(c + 1, i // 2, range(3) if c < 2 else range(2))

            def hidden_act(n):
                u, r = divmod(n, 4)
                ep = u % 4
                c, d = divmod(r, 2)
                col = 2 * (2 * ep + d) + c
                act.wait_ge(*filled("h", n))
                if n >= 4:
                    u0, c0 = divmod(n // 2 - 2, 2)
                    if c0:
                        act.wait_ge(*filled("e", u0))
                    else:
                        act.wait_ge(down_done, u0 + 1)
                b = n % 3
                A(HR[n % 4][:, :], PS[b][:, :], ACT.Gelu, bias=B1P[:, col:col + 1]).then_inc(bank_drained[b], 1)

            for t in range(18 + 4 * NG + 4):
                if t < NPAIR:
                    for tv in ([0, 1] if t == 0 else [t + 1]):
                        if tv >= NPAIR:
                            continue
                        if tv == 0:
                            act.wait_ge(bv_zeroed, 3)
                        if tv >= 3:
                            act.wait_ge(*filled("o", tv - 3))
                        act.wait_ge(*filled("v", tv))
                        for w in range(2):
                            last = A(BV[tv % 3][w * C:w * C + C, :, w, 0:HD],
                                     PS[6][w * C:w * C + C, 0:256].rearrange("p (h d) -> p h d", h=NH), ACT.Copy)
                        last.then_inc(bank_drained[6], 1)
                        if t == 0 and tv == 0:
                            continue
                    act.wait_ge(*drained("score", t))
                    if t >= 2 and (t - 2) % 4 == 3:
                        act.wait_ge(*filled("ss", (t - 2) // 4))
                    elif t >= 2:
                        act.wait_ge(sq_used, t - 1 - (t - 1) // 4)
                    A(SQ[t % 2][:, :], SR[t % 3][:, :], ACT.Square).then_inc(sq_ready, 1)
                    if t == 0:
                        for n in range(4):
                            spread(5, n, range(2))
                if 1 <= t <= NPAIR:
                    a = t - 1
                    if a == 0:
                        act.wait_ge(*filled("bd", 5, 3))
                    if a >= 8:
                        act.wait_ge(on_ready, 4 * (a // 4 - 1) )
                    act.wait_ge(*filled("o", a))
                    A(OR[:, a % 8, :, :, :].rearrange("p h w d -> p (h w d)"), PS[2 + a % 2][:, 0:264],
                      ACT.Copy).then_inc(bank_drained[2 + a % 2], 1)
                if 5 <= t and (t - 5) % 4 == 0 and (t - 5) // 4 < NG:
                    j = (t - 5) // 4
                    if j >= 1:
                        act.wait_ge(*filled("st", j - 1))
                    act.wait_ge(*filled("ss", j))
                    A(SSB[:, :], PS[4][:, :], ACT.Copy).then_inc(bank_drained[4], 1)
                j, r = divmod(t - 9, 4)
                if r == 0 and 0 <= j < NG:
                    for half in range(2):
                        act.wait_ge(*filled("on", j, half))
                        if half == 0 and j >= 1:
                            act.wait_ge(*filled("y", j - 1))
                        for q in range(2):
                            src = PS[5][:, 2 * q * P:2 * q * P + 2 * P].rearrange("p (w g o) -> p g w o", w=2, g=2)
                            last = A(ONT[:, 2 * half + q, :, :].rearrange("p g (w o) -> p g w o", w=2), src, ACT.Copy)
                        last.then_inc(bank_drained[5], 1)
                if 8 <= t < 16:
                    e = t - 8
                    if e % 4 == 0:
                        act.wait_ge(w1r_in, 32 * (e // 4 + 1))
                    A(W1H[:, e * HID:e * HID + HID], W1R[:, e % 4, :], ACT.Copy,
                      scale=LNG[:, e:e + 1]).then_inc(w1h_ready, 1)
                j, r = divmod(t - 11, 4)
                if r == 0 and 0 <= j < NG:
                    if j >= 1:
                        act.wait_ge(*filled("lg", j - 1))
                    act.wait_ge(*filled("zt", j))
                    A(ZT[:, :], PS[6][0:C, :], ACT.Copy).then_inc(bank_drained[6], 1)
                j, r = divmod(t - 12, 4)
                if r == 0 and 0 <= j < NG:
                    act.wait_ge(*filled("x2", j))
                    A(X2[:, 512 * j:512 * j + 512], PS[7][:, :], ACT.Copy).then_inc(x2hi_ready, 1)
                    act.wait_ge(lg_ready, j + 1)
                    A(PX[:, :, :], LG[:, :, :], ACT.Exp).then_inc(px_ready, 1)
                j, r = divmod(t - 13, 4)
                if r == 0 and 0 <= j < NG:
                    act.wait_ge(*filled("gt", j))
                    A(GT[:, 512 * j:512 * j + 512], PS[7][0:24, 0:256].bitcast(BF16),
                      ACT.Copy).then_inc(bank_drained[7], 1)
                u = t - 18
                if 0 <= u < 4 * NG:
                    if u >= 2:
                        act.wait_ge(*drained("e", u - 2))
                    if u == 0:
                        act.wait_ge(*filled("score", NPAIR - 1))
                    act.wait_ge(*filled("gb", u))
                    A(GB[u % 2][:, :], PS[5][:, :], ACT.Copy).then_inc(bank_drained[5], 1)
                    if u == 0:
                        act.wait_ge(b1p_ready, 1)
                    hidden_act(4 * u)
                    hidden_act(4 * u + 1)
                    hidden_act(4 * u + 2)
                    hidden_act(4 * u + 3)

        @block.vector
        def _(dve):
            n = [0]

            def step(ins):
                n[0] += 1
                ins.then_inc(dve_step, 1)
                dve.wait_ge(dve_step, n[0])

            V_ = nc.vector

            def moments(xin, xm, sq, j, eps):
                step(V_.tensor_reduce(S1[:, j, :], xin, AX.X, ALU.add))
                step(V_.tensor_scalar(S1[:, j, :], S1[:, j, :], 1.0 / C, None, ALU.mult))
                step(V_.tensor_tensor(xm, xin, S1[:, j, :].unsqueeze(2).to_broadcast([P, 4, C]), ALU.subtract))
                step(V_.tensor_tensor(sq, xm, xm, ALU.mult))
                step(V_.tensor_reduce(S2[:, j, :], sq, AX.X, ALU.add))
                V_.tensor_scalar(S2[:, j, :], S2[:, j, :], 1.0 / C, eps, ALU.mult, ALU.add).then_inc(var_ready, 1)

            def normalise(dst, xm, j, kind, dup):
                dve.wait_ge(rstd_ready, ask_no[(kind, j)])
                r = RS[:, j, :].unsqueeze(2)
                if dup:
                    return V_.tensor_tensor(dst, xm.unsqueeze(2).to_broadcast([P, 4, 2, C]),
                                            r.unsqueeze(3).to_broadcast([P, 4, 2, C]), ALU.mult)
                return V_.tensor_tensor(dst, xm, r.to_broadcast([P, 4, C]), ALU.mult)

            for j in range(NG):
                dve.wait_ge(x_in[j], 16)
                moments(XR[:, 4 * j:4 * j + 4, :], XM[:, 4 * j:4 * j + 4, :], XN[:, 4 * j:4 * j + 4, 0, :], j, EPS_C)
            dve.wait_ge(consts_ready, 2)
            for j in range(NG):
                normalise(XN[:, 4 * j:4 * j + 4, :, :], XM[:, 4 * j:4 * j + 4, :], j, "x", True).then_inc(xn_ready, 1)
            dve.wait_ge(whi_ready, 1)
            V_.tensor_tensor(WLO[:, :], WS[:, :], WHI[:, :].bitcast(F32), ALU.subtract).then_inc(wlo_ready, 1)
            dve.wait_ge(rel0_in, 16)
            for ij in range(WH):
                src = RB[:, :].rearrange("p (r c) -> p r c", c=SIDE)
                last = V_.tensor_copy(EB[:, ij, :, :], src[:, :, WH - 1 - ij:2 * WH - 1 - ij])
            last.then_inc(bias_rows, 1)
            for j in range(NG):
                dve.wait_ge(xhi_ready, j + 1)
                lo = XS[C:P, 8 * j:8 * j + 8, :].rearrange("p w o -> p (w o)")
                V_.tensor_tensor(lo, PS[j][C:P, :], lo.bitcast(F32), ALU.subtract).then_inc(bank_drained[j], 1)
            dve.wait_ge(rel_in, 16)
            for oj in range(WH):
                src = REL[:, 0, :, ::-1].rearrange("p g (y c) -> p g y c", c=SIDE)
                last = V_.tensor_copy(PN[:, :, oj, :, :], src[:, :, :, WH - 1 - oj:2 * WH - 1 - oj])
            last.then_inc(pn_ready, 1)
            dve.wait_ge(small_in, 16 * N_SMALL)
            dve.wait_ge(*filled("b1"))
            V_.tensor_tensor(B1P[:, :], PS[7][:, 0:16], B1[:, :], ALU.add).then_inc(bank_drained[7], 1)
            V_.tensor_tensor(XR[:, :, :], XR[:, :, :], BFB[:, :].unsqueeze(1).to_broadcast([P, NPAIR, C]),
                             ALU.add).then_inc(b1p_ready, 1)

            def spread(c, nn, heads):
                g, s = divmod(nn, 2)
                b = before[("bd", c, nn)][0]
                if nn == 0:
                    dve.wait_ge(bd_zeroed, c % 2 + 1)
                    if c >= 2:
                        dve.wait_ge(*filled("t", 8 * (c - 2) + 7))
                dve.wait_ge(*filled("bd", c, nn))
                for h in heads:
                    r = slice(HD * h, HD * h + HD)
                    bias = BP[r, 2 * KINDS[c] + g:2 * KINDS[c] + g + 1]
                    dst = BD[c % 2][r, g, h, :]
                    if KINDS[c] == Q:
                        last = V_.tensor_scalar(dst[:, 512 * s:512 * s + 512], PS[b][r, :], bias, None, ALU.add)
                    else:
                        dst = dst.rearrange("p (o w) -> p w o", w=NW)[:, 16 * s:16 * s + 16, :]
                        last = V_.tensor_scalar(dst, PS[b][r, :].rearrange("p (w o) -> p w o", w=16), bias, None,
                                                ALU.add)
                last.then_inc(bank_drained[b], 1)

            for c in range(2):
                for nn in range(4):
                    spread(c, nn, range(2, 4))
            dve.wait_ge(bias_in, 16 * 16)
            for c in range(4):
                for i in range(8):
                    tile = 8 * c + i
                    if c < 2:
                        o0 = 4 * tile
                        dve.wait_ge(*filled("t", tile))
                        for g in range(2):
                            r = slice(g * C, g * C + C)
                            for w in range(2):
                                src = PS[tile % 4][r, :].rearrange("p (o h t w) -> p w o h t", o=4, h=4, w=2)[:, w]
                                bias = BI[r, :, o0:o0 + 4].rearrange("p h o -> p o h").unsqueeze(3)
                                dst = TN[w * C:w * C + C, :, :, g, o0:o0 + 4].rearrange("p t h o -> p o h t")
                                last = V_.tensor_tensor(dst, src, bias.to_broadcast([C, 4, 4, NPAIR]), ALU.add)
                        last.then_inc(bank_drained[tile % 4], 1)
                    if c >= 1 and i % 2 == 0:
                        spread(c + 1, i // 2, range(3, 4) if c < 2 else range(2, 4))

            dve.wait_ge(b1p_ready, 1)
            dve.wait_ge(*drained("t", 15))
            for t in range(18 + 4 * NG + 8):
                u = t - 20
                if 0 <= u < 4 * NG:
                    j, ep = divmod(u, 4)
                    if ep == 0 and j >= 2:
                        dve.wait_ge(*filled("out", j - 2))
                    dve.wait_ge(*drained("gb", u))
                    dve.wait_ge(*filled("e", u))
                    if u >= 2:
                        dve.wait_ge(gate_done, u - 1 - (u - 1) // 4)
                    b = 3 + u % 2
                    dst = AC[j % 2] if ep == 0 else GM
                    ins = V_.scalar_tensor_tensor(out=dst[:, :], in0=PS[b][:, :], scalar=B2[:, ep:ep + 1],
                                                  in1=GB[u % 2][:, :], op0=ALU.add, op1=ALU.mult)
                    ins.then_inc(bank_drained[b], 1)
                    if ep:
                        dve.wait_ge(*drained("e", u))
                        V_.tensor_tensor(AC[j % 2][:, :], AC[j % 2][:, :], GM[:, :], ALU.add).then_inc(gate_done, 1)
                j, r = divmod(t - 24, 4)
                if r == 0 and 0 <= j < NG:
                    y = XR[:, 4 * j:4 * j + 4, :]
                    dve.wait_ge(*filled("out", j))
                    V_.tensor_tensor(y, PS[6][:, 0:256].rearrange("p (q c) -> p q c", q=4), y,
                                     ALU.add).then_inc(bank_drained[6], 1)
                if t < NPAIR:
                    if t == 0:
                        dve.wait_ge(*filled("t", 31))
                    if t >= 3:
                        dve.wait_ge(*filled("o", t - 3))
                        dve.wait_ge(sq_ready, t - 2)
                    dve.wait_ge(*filled("score", t))
                    dst = SR[t % 3][:, :]
                    V_.tensor_tensor(dst, PS[t % 2][:, :], TN[:, t, :, :, :].rearrange("p h g o -> p (h g o)"),
                                     ALU.add).then_inc(bank_drained[t % 2], 1)
                    if t == 0:
                        for nn in range(4):
                            spread(5, nn, range(2, 4))
                if 8 <= t < 16:
                    e = t - 8
                    dve.wait_ge(w1h_ready, e + 1)
                    cols = slice(e * HID, e * HID + HID)
                    V_.scalar_tensor_tensor(out=W1L[:, cols], in0=W1R[:, e % 4, :], scalar=LNG[:, e:e + 1],
                                            in1=W1H[:, cols].bitcast(F32), op0=ALU.mult,
                                            op1=ALU.subtract).then_inc(w1l_ready, 1)
                j, r = divmod(t - 6, 4)
                if r == 0 and 0 <= j < NG:
                    q0 = (4 * j) % 8
                    dve.wait_ge(*drained("o", 4 * j + 3))
                    dve.wait_ge(*filled("st", j))
                    sums = OR[:, q0:q0 + 4, :, :, HD]
                    step(V_.tensor_tensor(VA[:, :, :, :], sums, sums, ALU.mult))
                    ss = PS[5][:, :].rearrange("p (h q r) -> p q h r", h=4, q=4)[:, :, :, 0:2]
                    step(V_.tensor_scalar(VA[:, :, :, :], VA[:, :, :, :], -1.0 / WT, None, ALU.mult))
                    V_.tensor_tensor(VB[:, :, :, :], ss, VA[:, :, :, :], ALU.add).then_inc(bank_drained[5], 1)
                    dve.wait_ge(*drained("st", j))
                    step(V_.tensor_scalar(VB[:, :, :, :], VB[:, :, :, :], 0.0, 1.0 / (WT - 1), ALU.max, ALU.mult))
                    V_.tensor_scalar(VB[:, :, :, :], VB[:, :, :, :], EPS_S, None, ALU.add).then_inc(var_ready, 1)
                j, r = divmod(t - 8, 4)
                if r == 0 and 0 <= j < NG:
                    q0 = (4 * j) % 8
                    dve.wait_ge(rstd_ready, ask_no[("o", j)])
                    if j >= 1:
                        dve.wait_ge(*filled("on", j - 1, 1))
                    for q in range(4):
                        V_.tensor_tensor(ON[:, q, :, :, :].rearrange("p w h d -> p h w d"),
                                         OR[:, q0 + q, :, :, 0:HD],
                                         RSC[:, q, :, :].unsqueeze(3).to_broadcast([P, 4, 2, HD]),
                                         ALU.mult).then_inc(on_ready, 1)
                j, r = divmod(t - 9, 4)
                if r == 0 and 0 <= j < NG:
                    x1 = XR[:, 4 * j:4 * j + 4, :]
                    dve.wait_ge(*filled("y", j))
                    V_.tensor_tensor(x1, PS[7][:, 0:256].rearrange("p (q c) -> p q c", q=4), x1,
                                     ALU.add).then_inc(bank_drained[7], 1)
                    dve.wait_ge(*drained("y", j))
                    moments(x1, XMS[:, :, :], SQX[:, :, :], j, EPS_T)
                j, r = divmod(t - 10, 4)
                if r == 0 and 0 <= j < NG:
                    if j >= 1:
                        dve.wait_ge(*filled("zt", j - 1))
                    normalise(Z[:, :, :], XMS[:, :, :], j, "z", False).then_inc(z_ready, 1)
                    dve.wait_ge(z_ready, j + 1)
                    moments(Z[:, :, :], XMS[:, :, :], SQX[:, :, :], j, EPS_T)
                j, r = divmod(t - 11, 4)
                if r == 0 and 0 <= j < NG:
                    if j >= 1:
                        dve.wait_ge(*filled("x2", j - 1))
                    normalise(Z2[:, :, :, :], XMS[:, :, :], j, "z2", True).then_inc(z2_ready, 1)
                j, r = divmod(t - 12, 4)
                if r == 0 and 0 <= j < NG:
                    dve.wait_ge(*filled("lg", j))
                    last = V_.tensor_tensor(LG[:, :, :], PS[6][:, 0:32].rearrange("p (q e) -> p q e", q=4),
                                            BRB[:, :].unsqueeze(1).to_broadcast([P, 4, NE]), ALU.add)
                    last.then_inc(bank_drained[6], 1)
                    dve.wait_ge(*drained("lg", j))
                    step(V_.tensor_reduce(M1[:, :], LG[:, :, :], AX.X, ALU.max))
                    V_.tensor_tensor(LG[:, :, :], LG[:, :, :], M1[:, :].unsqueeze(2).to_broadcast([P, 4, NE]),
                                     ALU.subtract).then_inc(lg_ready, 1)
                    dve.wait_ge(x2hi_ready, j + 1)
                    lo = X2[C:P, 512 * j:512 * j + 512]
                    V_.tensor_tensor(lo, PS[7][C:P, :], lo.bitcast(F32), ALU.subtract).then_inc(bank_drained[7], 1)
                    dve.wait_ge(px_ready, j + 1)
                    step(V_.tensor_reduce(M1[:, :], PX[:, :, :], AX.X, ALU.add))
                    step(V_.reciprocal(M2[:, :], M1[:, :]))
                    step(V_.tensor_tensor(PR[:, :, :], PX[:, :, :], M2[:, :].unsqueeze(2).to_broadcast([P, 4, NE]),
                                          ALU.mult))
                    other = PR[:, :, :].unsqueeze(2).to_broadcast([P, 4, NE, NE])
                    own = PR[:, :, :].unsqueeze(3).to_broadcast([P, 4, NE, NE])
                    for q in range(4):
                        step(V_.tensor_tensor(CG[:, q], other[:, q], own[:, q], ALU.is_gt))
                        step(V_.tensor_tensor(CE[:, q], other[:, q], own[:, q], ALU.is_equal))
                    step(V_.tensor_tensor(CE[:, :, :, :], CE[:, :, :, :],
                                          TRI[:, :, :].unsqueeze(1).to_broadcast([P, 4, NE, NE]), ALU.mult))
                    step(V_.tensor_tensor(CG[:, :, :, :], CG[:, :, :, :], CE[:, :, :, :], ALU.add))
                    step(V_.tensor_reduce(LG[:, :, :], CG[:, :, :, :], AX.X, ALU.add))
                    step(V_.scalar_tensor_tensor(out=PR[:, :, :], in0=LG[:, :, :], scalar=1.5, in1=PR[:, :, :],
                                                 op0=ALU.is_lt, op1=ALU.mult))
                    step(V_.tensor_reduce(M1[:, :], PR[:, :, :], AX.X, ALU.add))
                    step(V_.reciprocal(M2[:, :], M1[:, :]))
                    step(V_.tensor_tensor(PR[:, :, :], PR[:, :, :], M2[:, :].unsqueeze(2).to_broadcast([P, 4, NE]),
                                          ALU.mult))
                    if j >= 1:
                        dve.wait_ge(*filled("gt", j - 1))
                    step(V_.tensor_copy(G3[:, :, 0, :], PR[:, :, :]))
                    step(V_.tensor_tensor(PR[:, :, :], PR[:, :, :], G3[:, :, 0, :], ALU.subtract))
                    step(V_.tensor_copy(G3[:, :, 1, :], PR[:, :, :]))
                    V_.tensor_tensor(G3[:, :, 2, :], PR[:, :, :], G3[:, :, 1, :], ALU.subtract).then_inc(g3_ready, 1)


def kernel(**inputs):
    import numpy as np
    import concourse.bacc as bacc
    from concourse.bass_utils import run_bass_kernel_spmd

    a = {k: np.asarray(v) for k, v in inputs.items()}
    rel = a["L0_conv_intrinsic"].reshape(2, 4, NREL, 1 + 2 * HD)
    arrays = {
        "x": a["x"].reshape(2, 4, WH, 2, 2, WH, C).transpose(4, 2, 5, 0, 1, 3, 6).reshape(P, NPAIR, C),
        "W_prep": a["L0_conv_W_prep"],
        "b_prep": a["L0_conv_b_prep"].reshape(10, P).T,
        "rel": rel[..., 1:].reshape(2, 4, NREL, 2, HD).transpose(1, 4, 3, 0, 2).reshape(P, 2, 2, NREL),
        "rel0": rel[..., 0].reshape(NH, NREL),
        "W_fin": a["L0_conv_W_fin"].reshape(2, P, C).transpose(1, 0, 2),
        "b_fin": a["L0_conv_b_fin"],
        "Wr": a["L0_ffn_Wr"],
        "br": a["L0_ffn_br"],
        "ln_g": a["L0_ffn_ln_g"].T,
        "ln_b": a["L0_ffn_ln_b"].T,
        "W1": a["L0_ffn_W1"].transpose(1, 0, 2),
        "b1": a["L0_ffn_b1"].reshape(2 * NE, P).T,
        "W2": a["L0_ffn_W2"].reshape(2 * NE, P, C).transpose(1, 0, 2),
        "b2": a["L0_ffn_b2"].reshape(4, P).T,
    }
    arrays = {k: np.ascontiguousarray(v) for k, v in arrays.items()}
    nc = bacc.Bacc("TRN2", target_bir_lowering=False, num_devices=1)
    args = [nc.dram_tensor(f"in_{k}", v.shape, mybir.dt.from_np(v.dtype), kind="ExternalInput").ap()
            for k, v in arrays.items()]
    out = nc.dram_tensor("out", (P, NPAIR, C), F32, kind="ExternalOutput").ap()
    metaformer_kernel(nc, *args, out)
    r = run_bass_kernel_spmd(nc, [{f"in_{k}": v for k, v in arrays.items()}], core_ids=[0])
    y = np.asarray(r.results[0]["out"]).reshape(2, WH, WH, 2, 4, 2, C)
    return np.ascontiguousarray(y.transpose(3, 4, 1, 5, 0, 2, 6).reshape(2, 32, 32, C))
```

```python
from contextlib import ExitStack

import concourse.bass as bass
from concourse import mybir

F32 = mybir.dt.float32
F32R = mybir.dt.float32r
I32 = mybir.dt.int32
BF16 = mybir.dt.bfloat16
ALU = mybir.AluOpType
ACT = mybir.ActivationFunctionType
AX = mybir.AxisListType

P = 128
C = 64
NH, HD = 8, 32
WH = 8
WT = WH * WH
NW = 32
NPAIR = NW // 2
NG = NPAIR // 4
TOK = NW * WT
SIDE = 2 * WH - 1
NREL = SIDE * SIDE
NE, HID = 8, 256
EPS_C, EPS_T, EPS_S = 1e-6, 1e-5, 1e-5
QN, Q, K_, KM, V = range(5)
LAG = 16
KINDS = [QN, QN, KM, KM, Q, Q]


def make_plan():
    plan = [(("b1",), 3, 1)] + [(("xt", j), (0, 1, 2, 7)[j], 1) for j in range(NG)]

    def prep(c, n):
        return [(("bd", c, n), 4 + n, 1 if c else 2)]

    for n in (0, 2, 1, 3):
        plan += prep(0, n)
    for n in range(4):
        plan += prep(1, n)
    for c in range(4):
        for i in range(8):
            plan += [(("t", 8 * c + i), i % 4, 2 if c < 2 else 1)]
            if i % 2 == 0:
                plan += prep(c + 2, i // 2)
            elif c == 1:
                plan += [(("xc", i // 2), 4 + (i // 2 + 2) % 4, 1)]
            elif c >= 2:
                plan += [(("k", i % 4 // 2, 2 * (c - 2) + i // 4), 4 + (i // 2 + 2) % 4, 1)]
    for step in range(LAG + NG * 4 + 2):
        plan += [(u, b, r) for u, b, r in pe_steps(step)]
    return plan


def pe_steps(t):
    s = []
    if t < NPAIR:
        if t == 0:
            s.append((("v", 0), 6, 1))
        s.append((("score", t), t % 2, 1))
        if t + 1 < NPAIR:
            s.append((("v", t + 1), 6, 1))
    if 1 <= t <= NPAIR:
        s.append((("o", t - 1), 2 + (t - 1) % 2, 1))
    if 2 <= t <= NPAIR + 1 and (t - 2) % 4 == 3:
        s.append((("ss", (t - 2) // 4), 4, 1))
    elif 2 <= t <= NPAIR + 1:
        s.append((("ss part", t - 2), 4, 0))
    for kind, lag, uses in (
            ("st", 6, [(("st",), 5, 1)]),
            ("zt", 14, [(("zt",), 6, 1)]),
            ("on", 10, [(("on", 0), 7, 1), (("on", 1), 5, 1)]),
            ("lg", 15, [(("lg",), 6, 1), (("x2",), 5, 1)]),
            ("y", 11, [(("y",), 7, 1)])):
        j, r = divmod(t - lag, 4)
        if r == 0 and 0 <= j < NG:
            s += [((use[0], j) + use[1:], bank, readers) for use, bank, readers in uses]
    u = t - LAG
    if 0 <= u < 4 * NG:
        s += [(("h", 4 * u), (4 * u) % 3, 1), (("h", 4 * u + 1), (4 * u + 1) % 3, 1)]
    if 1 <= u <= 4 * NG:
        s.append((("e", u - 1), 3 + (u - 1) % 2, 1))
    if 0 <= u < 4 * NG:
        s += [(("h", 4 * u + 2), (4 * u + 2) % 3, 1), (("h", 4 * u + 3), (4 * u + 3) % 3, 1)]
    if 1 <= u <= 4 * NG:
        s.append((("gb", u - 1), 5, 1))
    if 0 <= u < 4 * NG:
        s.append((("e part", u), 3 + u % 2, 0))
    j, r = divmod(t - 16, 4)
    if r == 0 and 0 <= j < NG:
        s.append((("gt", j), 6, 1))
    j, r = divmod(t - LAG - 5, 4)
    if r == 0 and 0 <= j < NG:
        s.append((("out", j), 6, 1))
    return s


def metaformer_kernel(nc, x, W_prep, b_prep, rel, rel0, W_fin, b_fin, Wr, br, ln_g, ln_b, W1, b1,
                      W2, b2, out):
    before, at_fill, at_drain = {}, {}, {}
    fills, drains = [0] * 8, [0] * 8
    open_part = {}
    for use, bank, readers in make_plan():
        if readers == 0:
            if bank not in open_part:
                open_part[bank] = drains[bank]
            before[use] = (bank, open_part[bank])
            continue
        before[use] = (bank, open_part.pop(bank, drains[bank]))
        fills[bank] += 1
        drains[bank] += readers
        at_fill[use], at_drain[use] = (bank, fills[bank]), (bank, drains[bank])

    with ExitStack() as ctx:
        sem = lambda name: ctx.enter_context(nc.semaphore(name))
        bank_filled = [sem(f"bank{b}_filled") for b in range(8)]
        bank_drained = [sem(f"bank{b}_drained") for b in range(8)]
        PS = [ctx.enter_context(nc.psum_tensor(f"PS{b}", [P, 512], F32)) for b in range(8)]

        def filled(*use):
            return bank_filled[at_fill[use][0]], at_fill[use][1]

        def drained(*use):
            return bank_drained[at_drain[use][0]], at_drain[use][1]

        base = 16640
        arena = ctx.enter_context(nc.sbuf_tensor("arena", [P, (229344 - base - 512) // 4], F32))
        cursor = [base]

        def sb(name, shape, dt=F32, at=None):
            size = 2 if dt == BF16 else 4
            for n in shape[1:]:
                size *= n
            size = -(-size // 32) * 32
            where = at if at is not None else cursor
            t = nc.alloc_sbuf_tensor_at(name, shape, dt, offset=where[0])
            where[0] += size
            return t

        XR = sb("XR", [P, NPAIR, C])
        W2s = sb("W2s", [P, 16, C])
        KT = sb("KT", [P, 2, TOK])
        XC = sb("XC", [P, TOK], F32R)
        WVH = sb("WVH", [P, 256], F32R)
        WVL = sb("WVL", [P, 256], F32R)
        WF = sb("WF", [P, 2, C])
        IDN = sb("IDN", [P, P])
        IDB = sb("IDB", [P, P], BF16)
        II = sb("II", [P, C])
        ONES2 = sb("ONES2", [P, 32])
        SEL = sb("SEL", [24, 4, P], BF16)
        TRI = sb("TRI", [P, NE, NE], BF16)
        BP = sb("BP", [P, 10])
        B1 = sb("B1", [P, 16])
        B1P = sb("B1P", [P, 16])
        B2 = sb("B2", [P, 4])
        LNG = sb("LNG", [P, NE])
        BRB = sb("BRB", [P, NE])
        WRs = sb("WRs", [C, NE])
        MV = sb("MV", [P, NPAIR, 2])
        RZ = sb("RZ", [P, 3, NG, 4])
        NHALF = sb("NHALF", [P, 32])
        BNS = sb("BNS", [P, 4, 6])
        tn_at = [cursor[0]]
        TN = sb("TN", [P, NPAIR, 4, 2, WT])
        tm_at = [cursor[0]]
        TM = sb("TM", [P, P, WT])
        bd_at = [[cursor[0]], [cursor[0] + 32768]]
        BD = [sb(f"BD{n}", [P, 2, 4, 1024]) for n in range(2)]
        region = cursor[0]

        XN = sb("XN", [P, NPAIR, 2, C], at=tm_at)
        CEN = sb("CEN", [P, P], at=tm_at)
        LNB = sb("LNB", [C, NE], at=tm_at)
        BFB = sb("BFB", [P, C], at=tm_at)
        RB = sb("RB", [NH, NREL], at=tm_at)
        EB = sb("EB", [NH, WH, SIDE, WH], at=tm_at)
        RS = sb("RS", [P, NPAIR], at=tm_at)
        VE = sb("VE", [P, NPAIR], at=tm_at)
        NB = sb("NB", [P, NPAIR], at=tm_at)
        RA = sb("RA", [P, NPAIR], at=tm_at)
        WS = sb("WS", [P, 1280], at=tm_at)
        REL = sb("REL", [P, 2, 2, NREL], at=tm_at)
        PN = sb("PN", [P, 2, WH, SIDE, WH], at=tm_at)
        W1E = sb("W1E", [C, NE * HID], at=tn_at)
        r_at = [region]
        WHI = sb("WHI", [P, 1024], F32R, at=r_at)
        WLO = sb("WLO", [P, 1024], F32R, at=r_at)
        XS = sb("XS", [P, NW, WT], F32R, at=r_at)
        ab_at = [r_at[0]]
        PM = sb("PM", [P, 2, WH, SIDE, WH], at=r_at)
        BI = sb("BI", [P, 4, WT], at=r_at)
        STG = [sb(f"STG{n}", [P, 2, 1024], at=r_at) for n in range(2)]
        late = [region]
        OR = sb("OR", [P, 8, 4, 2, HD + 1], at=late)
        ON = sb("ON", [P, 4, 2, 4, HD], at=late)
        ONT = sb("ONT", [P, 4, 2, P], at=late)
        VA = sb("VA", [P, 4, 4, 2], at=late)
        VB = sb("VB", [P, 4, 4, 2], at=late)
        RSC = sb("RSC", [P, 4, 4, 2], at=late)
        PX = sb("PX", [P, 4, NE], at=late)
        M1 = sb("M1", [P, 4], at=late)
        M2 = sb("M2", [P, 4], at=late)
        G3 = sb("G3", [P, 4, 3, NE], BF16, at=late)
        ab_at[0] = max(ab_at[0], late[0])
        SR = [sb(f"SR{n}", [P, 512], at=ab_at) for n in range(3)]
        SQ = [sb(f"SQ{n}", [P, 512], at=ab_at) for n in range(2)]
        BV = [sb(f"BV{n}", [P, NH, 2, HD + 1], at=ab_at) for n in range(3)]
        rest = [ab_at[0]]
        SSB = sb("SSB", [P, 512], at=rest)
        ZT = sb("ZT", [C, 512], at=rest)
        LG = sb("LG", [P, 4, NE], at=rest)
        PR = sb("PR", [P, 4, NE], at=rest)
        Z = sb("Z", [P, 4, C], at=rest)
        Z2 = sb("Z2", [P, 4, 2, C], at=rest)
        CG = sb("CG", [P, 4, NE, NE], at=rest)
        CE = sb("CE", [P, 4, NE, NE], BF16, at=rest)
        assert rest[0] <= 229344, rest
        W1H = sb("W1H", [P, NE * HID], F32R, at=bd_at[0])
        W1L = sb("W1L", [P, NE * HID], F32R, at=bd_at[0])
        X2 = sb("X2", [P, TOK], F32R, at=bd_at[0])
        W1R = sb("W1R", [P, 4, HID], at=bd_at[0])
        GT = sb("GT", [24, TOK], BF16, at=bd_at[0])
        HR = [sb(f"HR{n}", [P, 512], at=bd_at[1]) for n in range(4)]
        GB = [sb(f"GB{n}", [P, 512], at=bd_at[1]) for n in range(2)]
        AC = [sb(f"AC{n}", [P, 512], at=bd_at[1]) for n in range(2)]
        GM = sb("GM", [P, 512], at=bd_at[1])
        scratch = nc.dram_tensor("bias_rows", [NH, WH, SIDE * WH], F32).ap()

        x_in = [sem(f"x_in{j}") for j in range(NG)]
        wprep_in = sem("wprep_in")
        w1e_in = sem("w1e_in")
        lnb_in = sem("lnb_in")
        b1_in = sem("b1_in")
        rel_in = sem("rel_in")
        rel0_in = sem("rel0_in")
        small_in = sem("small_in")
        bias_out = sem("bias_out")
        bias_in = sem("bias_in")
        w1r_in = sem("w1r_in")
        result_out = sem("result_out")
        dve_step = sem("dve_step")
        act_step = sem("act_step")
        pool_step = sem("pool_step")
        consts_ready = sem("consts_ready")
        bd_zeroed = sem("bd_zeroed")
        bv_zeroed = sem("bv_zeroed")
        pm_ready = sem("pm_ready")
        pn_ready = sem("pn_ready")
        bias_rows = sem("bias_rows_ready")
        whi_ready = sem("whi_ready")
        wlo_ready = sem("wlo_ready")
        mv_ready = sem("mv_ready")
        rsc_ready = sem("rsc_ready")
        rz_ready = sem("rz_ready")
        wvh_ready = sem("wvh_ready")
        wvl_ready = sem("wvl_ready")
        xchi_ready = sem("xchi_ready")
        bd_in = [sem(f"bd_in{n}") for n in range(2)]
        rx_ready = sem("rx_ready")
        xn_ready = sem("xn_ready")
        xn2_ready = sem("xn2_ready")
        xhi_ready = sem("xhi_ready")
        sq_ready = sem("sq_ready")
        on_ready = sem("on_ready")
        z_ready = sem("z_ready")
        z2_ready = sem("z2_ready")
        x2hi_ready = sem("x2hi_ready")
        lg_ready = sem("lg_ready")
        px_ready = sem("px_ready")
        g3_ready = sem("g3_ready")
        w1h_ready = sem("w1h_ready")
        w1l_ready = sem("w1l_ready")
        down_done = sem("down_done")
        gate_done = sem("gate_done")
        sq_used = sem("sq_used")
        xb_ready = sem("xb_ready")

        def moved(c):
            return bd_in[c % 2], 4 * 16 * ((c + 1) // 2)

        block = ctx.enter_context(nc.Block())

        @block.sync
        def _(sp):
            for j in range(NG):
                sp.dma_start(XR[:, 4 * j:4 * j + 4, :], x[:, 4 * j:4 * j + 4, :]).then_inc(x_in[j], 16)
            sp.dma_start(W1E[:, :].rearrange("p (e h) -> p e h", e=NE), W1).then_inc(w1e_in, 16)
            sp.dma_start(WS[0:C, :], W_prep).then_inc(wprep_in, 16)
            sp.dma_start(WS[C:P, :], W_prep).then_inc(wprep_in, 16)
            sp.dma_start(B1[:, :], b1).then_inc(b1_in, 16)
            sp.dma_start(REL[:, :, :, :], rel).then_inc(rel_in, 16)
            for dst, src in ((BP[:, :], b_prep),
                             (B2[:, :], b2), (LNG[0:C, :], ln_g), (LNG[C:P, :], ln_g),
                             (BFB[:, :], b_fin.partition_broadcast(P)),
                             (BRB[:, :], br.partition_broadcast(P)), (WRs[:, :], Wr),
                             (WF[:, :, :], W_fin), (W2s[:, :, :], W2)):
                sp.dma_start(dst, src).then_inc(small_in, 16)
            for c in range(1, 6):
                for n in range(4):
                    sp.wait_ge(*drained("bd", c, n))
                if c == 1:
                    sp.wait_ge(bd_zeroed, 2)
                else:
                    sp.wait_ge(*filled("t", 8 * (c - 2) + 7))
                for h in range(4):
                    r = slice(HD * h, HD * h + HD)
                    sp.dma_start(BD[c % 2][r, :, h, :], STG[c % 2][r, :, :]).then_inc(bd_in[c % 2], 16)
                if c == 1:
                    sp.wait_ge(bias_rows, 1)
                    sp.dma_start(scratch, EB[:, :, :, :].rearrange("h j r c -> h j (r c)")).then_inc(bias_out, 16)
                    sp.wait_ge(bias_out, 16)
                    for g in range(2):
                        for oy in range(WH):
                            lo = (WH - 1 - oy) * WH
                            src = scratch[4 * g:4 * g + 4, :, lo:lo + WT].rearrange("h j i -> j h i")
                            r0 = g * C + oy * WH
                            sp.dma_start(BI[r0:r0 + WH, :, :], src).then_inc(bias_in, 16)
            sp.wait_ge(*filled("score", NPAIR // 2 - 1))
            for half in range(2):
                if half:
                    sp.wait_ge(w1l_ready, 4)
                for d in range(2):
                    sp.dma_start(W1R[d * C:d * C + C, :, :], W1[:, 4 * half:4 * half + 4, :]).then_inc(w1r_in, 16)
            for j in range(NG):
                sp.wait_ge(*drained("out", j))
                sp.dma_start(out[:, 4 * j:4 * j + 4, :], XR[:, 4 * j:4 * j + 4, :]).then_inc(result_out, 16)
            sp.wait_ge(result_out, 16 * NG)

        N_SMALL = 9

        @block.gpsimd
        def _(pool):
            n = [0]

            def step(ins):
                n[0] += 1
                ins.then_inc(pool_step, 1)
                pool.wait_ge(pool_step, n[0])

            pool.dma_start(LNB[:, :], ln_b).then_inc(lnb_in, 16)
            pool.dma_start(RB[:, :], rel0).then_inc(rel0_in, 16)
            step(pool.memset(IDN[:, :], 0.0))
            pool.affine_select(out=IDN[:, :], in_=IDN[:, :], compare_op=ALU.not_equal, fill=1.0, base=0,
                               pattern=[[-1, P]], channel_multiplier=1).then_inc(consts_ready, 1)
            step(pool.memset(NHALF[:, :], -0.5))
            step(pool.memset(CEN[:, :], 0.0))
            step(pool.memset(CEN[0:C, 0:C], -1.0 / WT))
            step(pool.memset(CEN[C:P, C:P], -1.0 / WT))
            pool.wait_ge(consts_ready, 1)
            pool.tensor_tensor(CEN[:, :], CEN[:, :], IDN[:, :], ALU.add).then_inc(consts_ready, 1)

            step(pool.memset(BD[0][:, 0, :, :], 0.0))
            pool.wait_ge(whi_ready, 1)
            nc.gpsimd.tensor_tensor(WLO[:, :], WS[:, 0:V * 256], WHI[:, :].bitcast(F32),
                                    ALU.subtract).then_inc(wlo_ready, 1)
            pool.wait_ge(wlo_ready, 1)
            pool.memset(BD[0][:, 1, :, :], 0.0).then_inc(bd_zeroed, 1)
            pool.memset(BD[1][:, :, :, :], 0.0).then_inc(bd_zeroed, 1)
            pool.wait_ge(rel_in, 16)
            for ij in range(WH):
                src = REL[:, 1, :, :].rearrange("p g (r c) -> p g r c", c=SIDE)
                pool.tensor_copy(PM[:, :, ij, :, :], src[:, :, :, WH - 1 - ij:2 * WH - 1 - ij]).then_inc(pm_ready, 1)
            pool.wait_ge(small_in, 16 * N_SMALL)
            pool.wait_ge(xn_ready, 2)
            pool.wait_ge(xn2_ready, 2)
            nc.gpsimd.tensor_tensor(XR[:, :, :], XR[:, :, :], BFB[:, :].unsqueeze(1).to_broadcast([P, NPAIR, C]),
                                    ALU.add).then_inc(xb_ready, 1)
            pool.wait_ge(xb_ready, 1)
            step(pool.memset(ONES2[:, :], 0.0))
            step(pool.memset(ONES2[0:C, 0:1], 1.0))
            step(pool.memset(ONES2[C:P, 1:2], 1.0))
            step(pool.memset(II[:, :], 0.0))
            for d in range(2):
                step(pool.affine_select(out=II[:, :], in_=II[:, :], compare_op=ALU.not_equal, fill=1.0,
                                        base=-C * d, pattern=[[-1, C]], channel_multiplier=1))
            step(pool.memset(SEL[:, :, :], 0.0))
            sel = SEL[:, :, :].rearrange("k p (d c) -> k p d c", d=2)
            for part in range(3):
                step(pool.affine_select(out=sel, in_=sel, compare_op=ALU.not_equal, fill=1.0, base=-NE * part,
                                        pattern=[[-2, 4], [-1, 2], [0, C]], channel_multiplier=1))
            step(pool.memset(TRI[:, :, :], 1.0))
            step(pool.affine_select(out=TRI[:, :, :], in_=TRI[:, :, :], compare_op=ALU.is_gt, fill=0.0, base=0,
                                    pattern=[[1, NE], [-1, NE]], channel_multiplier=0))
            pool.tensor_copy(IDB[:, :], IDN[:, :]).then_inc(consts_ready, 1)
            pool.wait_ge(*filled("t", 31))
            pool.wait_ge(*moved(4))
            for m, v in enumerate(BV):
                if m == 2:
                    pool.wait_ge(*moved(5))
                step(pool.memset(v[:, :, :, :], 0.0))
                step(pool.memset(v[0:C, :, 0, HD:HD + 1], 1.0))
                pool.memset(v[C:P, :, 1, HD:HD + 1], 1.0).then_inc(bv_zeroed, 1)
                pool.wait_ge(bv_zeroed, m + 1)
            G = nc.gpsimd
            for t in range(NPAIR + 12):
                j, r = divmod(t - 6, 4)
                if r == 0 and 0 <= j < NG:
                    pool.wait_ge(*drained("st", j))
                    vb = VB[:, :, :, :].rearrange("p q h g -> p (q h g)")
                    step(G.tensor_scalar(vb, vb, 0.0, 1.0 / (WT - 1), ALU.max, ALU.mult))
                    step(G.tensor_scalar(vb, vb, EPS_S, None, ALU.add))
                    if j >= 1:
                        pool.wait_ge(on_ready, 4 * j)
                    G.tensor_tensor(RSC[:, :, :, :].rearrange("p q h g -> p (q h g)"), vb, NHALF[:, :],
                                    ALU.pow).then_inc(rsc_ready, 1)
                j, r = divmod(t - 12, 4)
                if r == 0 and 0 <= j < NG:
                    pool.wait_ge(mv_ready, j + 1)
                    pool.wait_ge(rsc_ready, min(j + 2, NG))
                    v, r1, r2 = MV[:, 4 * j:4 * j + 4, 1], RZ[:, 0, j, :], RZ[:, 1, j, :]
                    work = RZ[:, 2, j, :]
                    step(G.tensor_scalar(work, v, EPS_T, None, ALU.add))
                    G.tensor_tensor(r1, work, NHALF[:, 0:4], ALU.pow).then_inc(rz_ready, 1)
                    pool.wait_ge(rz_ready, 2 * j + 1)
                    step(G.tensor_tensor(work, r1, r1, ALU.mult))
                    step(G.tensor_tensor(work, work, v, ALU.mult))
                    step(G.tensor_scalar(work, work, EPS_T, None, ALU.add))
                    G.tensor_tensor(r2, work, NHALF[:, 0:4], ALU.pow).then_inc(rz_ready, 1)
                    pool.wait_ge(rz_ready, 2 * j + 2)

        @block.tensor
        def _(pe):
            def begin(*use):
                bank, count = before[use]
                if count:
                    pe.wait_ge(bank_drained[bank], count)
                return PS[bank]

            def end(ins, *use):
                ins.then_inc(bank_filled[at_fill[use][0]], 1)

            def shift_bias(experts):
                for e in experts:
                    for c in range(2):
                        m = nc.tensor.matmul(PS[3][:, 2 * e + c:2 * e + c + 1],
                                             W1E[:, e * HID + c * P:e * HID + c * P + P],
                                             LNB[:, e:e + 1], start=True, stop=True)
                return m

            pe.wait_ge(w1e_in, 16)
            pe.wait_ge(lnb_in, 16)
            shift_bias(range(5))
            pe.wait_ge(consts_ready, 2)
            for j in range(NG):
                if j < 2:
                    pe.wait_ge(xn_ready, j + 1)
                else:
                    pe.wait_ge(xn2_ready, j - 1)
                ps = begin("xt", j)
                for n in range(4):
                    m = nc.tensor.transpose(ps[:, n * P:n * P + P],
                                            XN[:, 4 * j + n, :, :].rearrange("p d c -> p (d c)"), IDN[:, :])
                end(m, "xt", j)

            def centred(j):
                ps = begin("xc", j)
                for n in range(4):
                    m = nc.tensor.matmul(ps[:, n * P:n * P + P],
                                         XN[:, 4 * j + n, :, :].rearrange("p d c -> p (d c)"), CEN[:, :],
                                         start=True, stop=True)
                end(m, "xc", j)

            def keys(g, s):
                ps = begin("k", g, s)
                end(project(ps, K_, g, XS[:, 8 * s:8 * s + 8, :]), "k", g, s)

            def project(ps, kind, g, moving):
                col = kind * 256 + g * P
                nc.tensor.matmul(ps[:, :], WHI[:, col:col + P], moving, start=True, stop=False)
                return nc.tensor.matmul(ps[:, :], WLO[:, col:col + P], moving, start=False, stop=True)

            pe.wait_ge(whi_ready, 1)
            pe.wait_ge(wlo_ready, 1)
            def prep(c, n):
                g, s = divmod(n, 2)
                half = c % 2
                if KINDS[c] == Q:
                    w0 = 16 * half + 8 * s
                    moving = XS[:, w0:w0 + 8, :]
                else:
                    moving = XS[:, 16 * s:16 * s + 16, 32 * half:32 * half + 32]
                ps = begin("bd", c, n)
                end(project(ps, KINDS[c], g, moving), "bd", c, n)

            def pattern(tile):
                c, i = divmod(tile, 8)
                table = PN if c < 2 else PM
                slot = BD[c % 2]
                if tile == 0:
                    for n in range(4):
                        pe.wait_ge(*drained("bd", 0, n))
                elif i == 0:
                    pe.wait_ge(*moved(c))
                ps = begin("t", tile)
                for u in range(4):
                    local = 4 * i + u
                    fy, fx = divmod(32 * (c % 2) + local, WH)
                    for g in range(2):
                        rows = table[:, g, fx, WH - 1 - fy:2 * WH - 1 - fy, :].rearrange("p a b -> p (a b)")
                        moving = slot[:, g, :, 32 * local:32 * local + 32]
                        m = nc.tensor.matmul(ps[g * C:g * C + C, u * P:u * P + P], rows, moving,
                                             start=True, stop=True)
                end(m, "t", tile)

            for n in (0, 2, 1, 3):
                if n < 2:
                    pe.wait_ge(*drained("xt", 2 * n))
                    pe.wait_ge(*drained("xt", 2 * n + 1))
                prep(0, n)
            end(shift_bias(range(5, NE)), "b1")
            for n in range(4):
                prep(1, n)
            pe.wait_ge(pn_ready, 1)
            for c in range(4):
                if c == 2:
                    pe.wait_ge(pm_ready, WH)
                for i in range(8):
                    pattern(8 * c + i)
                    if i % 2 == 0:
                        prep(c + 2, i // 2)
                    elif c == 1:
                        centred(i // 2)
                    elif c >= 2:
                        keys(i % 4 // 2, 2 * (c - 2) + i // 4)

            def values(t):
                ps = begin("v", t)
                nc.tensor.matmul(ps[:, 0:256], XC[:, t * P:t * P + P], WVH[:, :], start=True, stop=False)
                end(nc.tensor.matmul(ps[:, 0:256], XC[:, t * P:t * P + P], WVL[:, :], start=False, stop=True), "v", t)

            def score(t):
                if t == 0:
                    pe.wait_ge(*drained("t", 31))
                    pe.wait_ge(*drained("k", 1, NG - 1))
                    pe.wait_ge(*moved(4))
                if t == NPAIR // 2:
                    pe.wait_ge(*moved(5))
                slot = BD[t // (NPAIR // 2)]
                ps = begin("score", t)
                for h in range(4):
                    pair = TM[:, h * NW + 2 * t:h * NW + 2 * t + 2, :].rearrange("p w i -> p (w i)")
                    nc.tensor.matmul(ps[:, h * P:h * P + P], pair, IDN[:, :], start=(h == 0), stop=False,
                                     is_transpose=True, skip_group_check=True)
                for g in range(2):
                    for w in range(2):
                        lo = (2 * t + w) * WT
                        lq = lo % 1024
                        dst = ps[w * C:w * C + C, :].rearrange("p (h g o) -> p h g o", h=4, g=2)[:, :, g, :]
                        m = nc.tensor.matmul(dst, KT[:, g, lo:lo + WT], slot[:, g, :, lq:lq + WT],
                                             start=False, stop=True, skip_group_check=True)
                end(m, "score", t)

            def weighted(t):
                pe.wait_ge(*drained("score", t))
                pe.wait_ge(*drained("v", t))
                ps = begin("o", t)
                for h in range(4):
                    for g in range(2):
                        dst = ps[g * C:g * C + C, h * 66:h * 66 + 66]
                        m = nc.tensor.matmul(dst, SR[t % 3][:, (2 * h + g) * C:(2 * h + g) * C + C],
                                             BV[t % 3][:, 4 * g + h, :, :].rearrange("p w d -> p (w d)"),
                                             start=True, stop=True)
                end(m, "o", t)

            def squares(t):
                q = t % 4
                pe.wait_ge(sq_ready, t + 1)
                last = q == 3
                ps = begin("ss", t // 4) if last else begin("ss part", t)
                m = nc.tensor.matmul(ps[32 * q:32 * q + 32, :], ONES2[:, :], SQ[t % 2][:, :], start=True, stop=True)
                m.then_inc(bank_filled[4] if last else sq_used, 1)

            def hidden(n):
                u, r = divmod(n, 4)
                j, ep = divmod(u, 4)
                c, d = divmod(r, 2)
                col = (2 * ep + d) * HID + c * P
                ps = begin("h", n)
                nc.tensor.matmul(ps[:, :], W1H[:, col:col + P], X2[:, j * 512:j * 512 + 512], start=True, stop=False)
                end(nc.tensor.matmul(ps[:, :], W1L[:, col:col + P], X2[:, j * 512:j * 512 + 512],
                                     start=False, stop=True), "h", n)

            def down(u, c):
                ep = u % 4
                pe.wait_ge(*drained("h", 4 * u + 2 * c))
                pe.wait_ge(*drained("h", 4 * u + 2 * c + 1))
                ps = begin("e part", u) if c == 0 else PS[before[("e", u)][0]]
                for d in range(2):
                    m = nc.tensor.matmul(ps[d * C:d * C + C, :], W2s[:, 2 * (2 * ep + d) + c, :],
                                         HR[(2 * c + d) % 4][:, :], start=(c == 0), stop=(c == 1),
                                         skip_group_check=True)
                m.then_inc(down_done if c == 0 else bank_filled[before[("e", u)][0]], 1)

            for t in range(LAG + 4 * NG + 2):
                for use, _, _ in pe_steps(t):
                    kind, a = use[0], use[1]
                    if kind == "v":
                        if a == 0:
                            pe.wait_ge(wvh_ready, 1)
                            pe.wait_ge(wvl_ready, 1)
                            pe.wait_ge(*drained("xc", NG - 1))
                        values(a)
                    elif kind == "score":
                        score(a)
                    elif kind == "o":
                        if a < 3:
                            pe.wait_ge(bv_zeroed, a + 1)
                        weighted(a)
                    elif kind == "ss part":
                        if a == 0:
                            pe.wait_ge(consts_ready, 3)
                        squares(a)
                    elif kind == "ss":
                        squares(4 * a + 3)
                    elif kind == "st":
                        pe.wait_ge(*drained("ss", a))
                        ps = begin("st", a)
                        for h in range(4):
                            m = nc.tensor.transpose(ps[:, h * P:h * P + P], SSB[:, h * P:h * P + P], IDN[:, :])
                        end(m, "st", a)
                    elif kind == "on":
                        half = use[2]
                        pe.wait_ge(on_ready, 4 * a + 2 * half + 2)
                        ps = begin("on", a, half)
                        for q in range(2):
                            for w in range(2):
                                m = nc.tensor.transpose(ps[:, (2 * q + w) * P:(2 * q + w) * P + P],
                                                        ON[:, 2 * half + q, w, :, :].rearrange("p h d -> p (h d)"),
                                                        IDN[:, :])
                        end(m, "on", a, half)
                    elif kind == "y":
                        if a == 0:
                            pe.wait_ge(small_in, 16 * N_SMALL)
                        pe.wait_ge(*drained("on", a, 1))
                        ps = begin("y", a)
                        for q in range(4):
                            for g in range(2):
                                m = nc.tensor.matmul(ps[:, q * C:q * C + C], ONT[:, q, g, :], WF[:, g, :],
                                                     start=(g == 0), stop=(g == 1))
                        end(m, "y", a)
                    elif kind == "zt":
                        pe.wait_ge(z_ready, a + 1)
                        ps = begin("zt", a)
                        for q in range(4):
                            m = nc.tensor.transpose(ps[0:C, q * P:q * P + P], Z[:, q, :], IDN[:, :])
                        end(m, "zt", a)
                    elif kind == "lg":
                        pe.wait_ge(*drained("zt", a))
                        ps = begin("lg", a)
                        for q in range(4):
                            m = nc.tensor.matmul(ps[:, q * NE:q * NE + NE], ZT[:, q * P:q * P + P], WRs[:, :],
                                                 start=True, stop=True)
                        end(m, "lg", a)
                    elif kind == "x2":
                        pe.wait_ge(z2_ready, a + 1)
                        ps = begin("x2", a)
                        for q in range(4):
                            m = nc.tensor.transpose(ps[:, q * P:q * P + P],
                                                    Z2[:, q, :, :].rearrange("p d c -> p (d c)"), IDN[:, :])
                        end(m, "x2", a)
                    elif kind == "gt":
                        pe.wait_ge(g3_ready, a + 1)
                        ps = begin("gt", a)
                        half_words = ps[0:24, 0:256].bitcast(BF16)
                        for q in range(4):
                            m = nc.tensor.transpose(half_words[:, q * P:q * P + P],
                                                    G3[:, q, :, :].rearrange("p k e -> p (k e)"), IDB[:, :])
                        end(m, "gt", a)
                    elif kind == "gb":
                        if a % 4 == 0:
                            pe.wait_ge(*drained("gt", a // 4))
                        ps = begin("gb", a)
                        end(nc.tensor.matmul(ps[:, :], SEL[:, a % 4, :], GT[:, (a // 4) * 512:(a // 4) * 512 + 512],
                                             start=True, stop=True), "gb", a)
                    elif kind == "h":
                        if a == 0:
                            pe.wait_ge(w1h_ready, NE)
                            pe.wait_ge(w1l_ready, NE)
                        if a % 16 == 0:
                            pe.wait_ge(*drained("x2", a // 16))
                        hidden(a)
                    elif kind == "e part":
                        down(a, 0)
                    elif kind == "e":
                        down(a, 1)
                    elif kind == "out":
                        pe.wait_ge(gate_done, 3 * a + 3)
                        ps = begin("out", a)
                        for q in range(4):
                            m = nc.tensor.matmul(ps[:, q * C:q * C + C], AC[a % 2][:, q * P:q * P + P], II[:, :],
                                                 start=True, stop=True)
                        end(m, "out", a)

        def weight_steps(t):
            return {9: (0, 1), 10: (2, 3), 13: (4, 5), 14: (6, 7)}.get(t, ())

        def twice(x):
            return x.unsqueeze(1).to_broadcast([P, 2, C])

        def token_order(c, dst):
            return dst if KINDS[c] == Q else dst.rearrange("p (o w) -> p w o", w=NW)

        def spread_first(engine, add, heads):
            engine.wait_ge(bd_zeroed, 1)
            for n in (0, 2, 1, 3):
                g, s = divmod(n, 2)
                engine.wait_ge(*filled("bd", 0, n))
                for h in heads:
                    r = slice(HD * h, HD * h + HD)
                    dst = token_order(0, BD[0][r, g, h, :])[:, 16 * s:16 * s + 16, :]
                    last = add(dst, PS[4 + n][r, :].rearrange("p (w o) -> p w o", w=16),
                               BP[r, 2 * KINDS[0] + g:2 * KINDS[0] + g + 1])
                last.then_inc(bank_drained[4 + n], 1)

        def stage(engine, add, c, n):
            g, s = divmod(n, 2)
            if c >= 3:
                engine.wait_ge(*moved(c - 2))
            engine.wait_ge(*filled("bd", c, n))
            bias = BP[:, 2 * KINDS[c] + g:2 * KINDS[c] + g + 1]
            if KINDS[c] == Q:
                last = add(STG[c % 2][:, g, 512 * s:512 * s + 512], PS[4 + n][:, :], bias)
            else:
                last = add(token_order(c, STG[c % 2][:, g, :])[:, 16 * s:16 * s + 16, :],
                           PS[4 + n][:, :].rearrange("p (w o) -> p w o", w=16), bias)
            last.then_inc(bank_drained[4 + n], 1)

        def move_tn(engine, copy, tile, g):
            o0 = 4 * tile
            engine.wait_ge(*filled("t", tile))
            for w in range(2):
                src = PS[tile % 4][g * C:g * C + C, :].rearrange("p (o h t w) -> p w o h t", o=4, h=4, w=2)[:, w]
                last = copy(TN[w * C:w * C + C, :, :, g, o0:o0 + 4].rearrange("p t h o -> p o h t"), src)
            last.then_inc(bank_drained[tile % 4], 1)

        @block.scalar
        def _(act):
            A = nc.scalar.activation

            def act_spread(dst, src, bias):
                return A(dst, src, ACT.Identity, bias=bias)

            act.wait_ge(wprep_in, 32)
            A(WHI[:, :], WS[:, 0:V * 256], ACT.Copy).then_inc(whi_ready, 1)
            act.wait_ge(rx_ready, 1)
            for j in range(2, NG):
                for n in range(4 * j, 4 * j + 4):
                    last = A(XN[:, n, :, :], twice(XR[:, n, :]), ACT.Identity, scale=RS[:, n:n + 1], bias=NB[:, n:n + 1])
                last.then_inc(xn2_ready, 1)
            for j in range(NG):
                act.wait_ge(*filled("xt", j))
                A(XS[:, 8 * j:8 * j + 8, :].rearrange("p w o -> p (w o)"), PS[before[("xt", j)][0]][:, :],
                  ACT.Copy).then_inc(xhi_ready, 1)
            act.wait_ge(small_in, 16 * N_SMALL)
            spread_first(act, act_spread, range(2))
            for n in range(0, 4, 2):
                stage(act, act_spread, 1, n)
            A(WVH[:, :], WS[:, V * 256:], ACT.Copy).then_inc(wvh_ready, 1)
            for tile in range(32):
                c, i = divmod(tile, 8)
                if c < 2:
                    move_tn(act, lambda dst, src: A(dst, src, ACT.Copy), tile, 0)
                if i % 2 == 0:
                    stage(act, act_spread, c + 2, i // 2)
                    continue
                b = 4 + (i // 2 + 2) % 4
                if c == 1:
                    j = i // 2
                    act.wait_ge(*filled("xc", j))
                    A(XC[:, 512 * j:512 * j + 512], PS[b][:, :], ACT.Copy).then_inc(xchi_ready, 1)
                elif c >= 2:
                    g, s = i % 4 // 2, 2 * (c - 2) + i // 4
                    act.wait_ge(*filled("k", g, s))
                    A(KT[:, g, 512 * s:512 * s + 512], PS[b][:, :], ACT.Identity,
                      bias=BP[:, 2 * K_ + g:2 * K_ + g + 1]).then_inc(bank_drained[b], 1)

            def hidden_act(n):
                u, r = divmod(n, 4)
                ep = u % 4
                c, d = divmod(r, 2)
                col = 2 * (2 * ep + d) + c
                act.wait_ge(*filled("h", n))
                if n >= 4:
                    u0, c0 = divmod(n // 2 - 2, 2)
                    if c0:
                        act.wait_ge(*filled("e", u0))
                    else:
                        act.wait_ge(down_done, u0 + 1)
                b = n % 3
                A(HR[n % 4][:, :], PS[b][:, :], ACT.Gelu, bias=B1P[:, col:col + 1]).then_inc(bank_drained[b], 1)

            for t in range(LAG + 4 * NG + 1):
                if t < NPAIR:
                    for tv in ([0, 1] if t == 0 else [t + 1]):
                        if tv >= NPAIR:
                            continue
                        if tv < 3:
                            act.wait_ge(bv_zeroed, tv + 1)
                        else:
                            act.wait_ge(*filled("o", tv - 3))
                        act.wait_ge(*filled("v", tv))
                        for w in range(2):
                            last = A(BV[tv % 3][w * C:w * C + C, :, w, 0:HD],
                                     PS[6][w * C:w * C + C, 0:256].rearrange("p (h d) -> p h d", h=NH), ACT.Copy)
                        last.then_inc(bank_drained[6], 1)
                        if t == 0 and tv == 0:
                            continue
                    act.wait_ge(*drained("score", t))
                    if t >= 2 and (t - 2) % 4 == 3:
                        act.wait_ge(*filled("ss", (t - 2) // 4))
                    elif t >= 2:
                        act.wait_ge(sq_used, t - 1 - (t - 1) // 4)
                    A(SQ[t % 2][:, :], SR[t % 3][:, :], ACT.Square).then_inc(sq_ready, 1)
                if 1 <= t <= NPAIR:
                    a = t - 1
                    if a == 0:
                        act.wait_ge(*filled("bd", 5, 3))
                    if a >= 8:
                        act.wait_ge(on_ready, a - 7)
                    act.wait_ge(*filled("o", a))
                    A(OR[:, a % 8, :, :, :].rearrange("p h w d -> p (h w d)"), PS[2 + a % 2][:, 0:264],
                      ACT.Copy).then_inc(bank_drained[2 + a % 2], 1)
                if 5 <= t and (t - 5) % 4 == 0 and (t - 5) // 4 < NG:
                    j = (t - 5) // 4
                    if j >= 1:
                        act.wait_ge(*filled("st", j - 1))
                    else:
                        act.wait_ge(*moved(5))
                    act.wait_ge(*filled("ss", j))
                    A(SSB[:, :], PS[4][:, :], ACT.Copy).then_inc(bank_drained[4], 1)
                j, r = divmod(t - 10, 4)
                if r == 0 and 0 <= j < NG:
                    for half in range(2):
                        act.wait_ge(*filled("on", j, half))
                        if half == 0 and j >= 1:
                            act.wait_ge(*filled("y", j - 1))
                        for q in range(2):
                            src = PS[7 - 2 * half][:, 2 * q * P:2 * q * P + 2 * P].rearrange("p (w g o) -> p g w o", w=2, g=2)
                            last = A(ONT[:, 2 * half + q, :, :].rearrange("p g (w o) -> p g w o", w=2), src, ACT.Copy)
                        last.then_inc(bank_drained[7 - 2 * half], 1)
                for e in weight_steps(t):
                    if e % 4 == 0:
                        act.wait_ge(w1r_in, 32 * (e // 4 + 1))
                    A(W1H[:, e * HID:e * HID + HID], W1R[:, e % 4, :], ACT.Copy,
                      scale=LNG[:, e:e + 1]).then_inc(w1h_ready, 1)
                j, r = divmod(t - 14, 4)
                if r == 0 and 0 <= j < NG:
                    if j >= 1:
                        act.wait_ge(*filled("lg", j - 1))
                    act.wait_ge(*filled("zt", j))
                    A(ZT[:, :], PS[6][0:C, :], ACT.Copy).then_inc(bank_drained[6], 1)
                j, r = divmod(t - 15, 4)
                if r == 0 and 0 <= j < NG:
                    act.wait_ge(*filled("x2", j))
                    A(X2[:, 512 * j:512 * j + 512], PS[5][:, :], ACT.Copy).then_inc(x2hi_ready, 1)
                    act.wait_ge(lg_ready, j + 1)
                    A(PX[:, :, :], LG[:, :, :], ACT.Exp).then_inc(px_ready, 1)
                u = t - LAG
                if 0 <= u < 4 * NG:
                    if u == 0:
                        act.wait_ge(*filled("score", NPAIR - 1))
                        act.wait_ge(*drained("b1"))
                    for n in range(4 * u, 4 * u + 4):
                        hidden_act(n)
                if 1 <= u <= 4 * NG:
                    if u >= 3:
                        act.wait_ge(*drained("e", u - 3))
                    act.wait_ge(*filled("gb", u - 1))
                    A(GB[(u - 1) % 2][:, :], PS[5][:, :], ACT.Copy).then_inc(bank_drained[5], 1)
                j, r = divmod(t - 16, 4)
                if r == 0 and 0 <= j < NG:
                    act.wait_ge(*filled("gt", j))
                    A(GT[:, 512 * j:512 * j + 512], PS[6][0:24, 0:256].bitcast(BF16),
                      ACT.Copy).then_inc(bank_drained[6], 1)

        @block.vector
        def _(dve):
            n = [0]

            def step(ins):
                n[0] += 1
                ins.then_inc(dve_step, 1)
                dve.wait_ge(dve_step, n[0])

            V_ = nc.vector

            def inverse_root(y, v, work):
                step(V_.tensor_scalar(y.bitcast(I32), v.bitcast(I32), -0.5, float(0x5F3759DF), ALU.mult, ALU.add))
                for _ in range(3):
                    step(V_.scalar_tensor_tensor(out=work, in0=y, scalar=-0.5, in1=y, op0=ALU.mult, op1=ALU.mult))
                    step(V_.tensor_tensor(work, work, v, ALU.mult))
                    step(V_.scalar_tensor_tensor(out=y, in0=work, scalar=1.5, in1=y, op0=ALU.add, op1=ALU.mult))

            def moments(xin, j):
                for q in range(4):
                    last = V_.bn_stats(BNS[:, q, :], xin[:, q, :])
                step(last)
                for q in range(4):
                    last = V_.bn_aggr(MV[:, 4 * j + q, :], BNS[:, q, :])
                return last

            def normalise(dst, xin, root, j):
                for q in range(4):
                    last = V_.tensor_scalar(dst(q), xin(q), MV[:, 4 * j + q, 0:1], root(q), ALU.subtract, ALU.mult)
                return last

            for j in range(NG):
                dve.wait_ge(x_in[j], 16)
                step(moments(XR[:, 4 * j:4 * j + 4, :], j))
            step(V_.tensor_scalar(VE[:, :], MV[:, :, 1], EPS_C, None, ALU.add))
            inverse_root(RS[:, :], VE[:, :], RA[:, :])
            V_.scalar_tensor_tensor(out=NB[:, :], in0=MV[:, :, 0], scalar=-1.0, in1=RS[:, :], op0=ALU.mult,
                                    op1=ALU.mult).then_inc(rx_ready, 1)
            for j in range(2):
                normalise(lambda q: XN[:, 4 * j + q, :, :], lambda q: twice(XR[:, 4 * j + q, :]),
                          lambda q: RS[:, 4 * j + q:4 * j + q + 1], j).then_inc(xn_ready, 1)
            dve.wait_ge(rel_in, 16)
            for oj in range(WH):
                src = REL[:, 0, :, ::-1].rearrange("p g (y c) -> p g y c", c=SIDE)
                last = V_.tensor_copy(PN[:, :, oj, :, :], src[:, :, :, WH - 1 - oj:2 * WH - 1 - oj])
            last.then_inc(pn_ready, 1)
            dve.wait_ge(rel0_in, 16)
            for oj in range(WH):
                src = RB[:, ::-1].rearrange("p (y c) -> p y c", c=SIDE)
                last = V_.tensor_copy(EB[:, oj, :, :], src[:, :, WH - 1 - oj:2 * WH - 1 - oj])
            last.then_inc(bias_rows, 1)
            for j in range(NG):
                dve.wait_ge(xhi_ready, j + 1)
                lo = XS[C:P, 8 * j:8 * j + 8, :].rearrange("p w o -> p (w o)")
                b = before[("xt", j)][0]
                V_.tensor_tensor(lo, PS[b][C:P, :], lo.bitcast(F32), ALU.subtract).then_inc(bank_drained[b], 1)
            def dve_spread(dst, src, bias):
                return V_.tensor_scalar(dst, src, bias, None, ALU.add)

            dve.wait_ge(small_in, 16 * N_SMALL)
            spread_first(dve, dve_spread, range(2, 4))
            for nn in range(1, 4, 2):
                stage(dve, dve_spread, 1, nn)
            dve.wait_ge(b1_in, 16)
            dve.wait_ge(*filled("b1"))
            V_.tensor_tensor(B1P[:, :], PS[3][:, 0:16], B1[:, :], ALU.add).then_inc(bank_drained[3], 1)
            dve.wait_ge(wvh_ready, 1)
            V_.tensor_tensor(WVL[:, :], WS[:, V * 256:], WVH[:, :].bitcast(F32), ALU.subtract).then_inc(wvl_ready, 1)
            for c in range(4):
                for i in range(8):
                    tile = 8 * c + i
                    if c < 2:
                        move_tn(dve, V_.tensor_copy, tile, 1)
                        if c == 1 and i % 2:
                            j = i // 2
                            b = 4 + (j + 2) % 4
                            dve.wait_ge(xchi_ready, j + 1)
                            lo = XC[C:P, 512 * j:512 * j + 512]
                            V_.tensor_tensor(lo, PS[b][C:P, :], lo.bitcast(F32),
                                             ALU.subtract).then_inc(bank_drained[b], 1)
                    else:
                        i0 = 4 * (tile - 16)
                        if tile == 16:
                            dve.wait_ge(xb_ready, 1)
                            dve.wait_ge(bias_in, 16 * 16)
                            dve.wait_ge(*filled("t", 15))
                            dve.wait_ge(wvl_ready, 1)
                        dve.wait_ge(*filled("t", tile))
                        bias = BI[:, :, i0:i0 + 4].rearrange("p h i -> p i h").unsqueeze(3)
                        V_.tensor_tensor(TM[:, :, i0:i0 + 4].rearrange("p (h w) i -> p i h w", h=4),
                                         PS[tile % 4][:, :].rearrange("p (i h w) -> p i h w", i=4, h=4),
                                         bias.to_broadcast([P, 4, 4, NW]), ALU.add)\
                            .then_inc(bank_drained[tile % 4], 1)

            dve.wait_ge(*drained("t", 15))
            for t in range(LAG + 4 * NG + 3):
                u = t - LAG - 2
                if 0 <= u < 4 * NG:
                    j, ep = divmod(u, 4)
                    if ep == 0 and j >= 2:
                        dve.wait_ge(*filled("out", j - 2))
                    dve.wait_ge(*drained("gb", u))
                    dve.wait_ge(*filled("e", u))
                    if u >= 2:
                        dve.wait_ge(gate_done, u - 1 - (u - 1) // 4)
                    b = 3 + u % 2
                    dst = AC[j % 2] if ep == 0 else GM
                    ins = V_.scalar_tensor_tensor(out=dst[:, :], in0=PS[b][:, :], scalar=B2[:, ep:ep + 1],
                                                  in1=GB[u % 2][:, :], op0=ALU.add, op1=ALU.mult)
                    ins.then_inc(bank_drained[b], 1)
                    if ep:
                        dve.wait_ge(*drained("e", u))
                        V_.tensor_tensor(AC[j % 2][:, :], AC[j % 2][:, :], GM[:, :], ALU.add).then_inc(gate_done, 1)
                j, r = divmod(t - LAG - 6, 4)
                if r == 0 and 0 <= j < NG:
                    y = XR[:, 4 * j:4 * j + 4, :]
                    dve.wait_ge(*filled("out", j))
                    V_.tensor_tensor(y, PS[6][:, 0:256].rearrange("p (q c) -> p q c", q=4), y,
                                     ALU.add).then_inc(bank_drained[6], 1)
                if t < NPAIR:
                    if t == 0:
                        dve.wait_ge(*filled("t", 31))
                        dve.wait_ge(*moved(4))
                    if t >= 3:
                        dve.wait_ge(*filled("o", t - 3))
                        dve.wait_ge(sq_ready, t - 2)
                    dve.wait_ge(*filled("score", t))
                    dst = SR[t % 3][:, :]
                    V_.tensor_tensor(dst, PS[t % 2][:, :], TN[:, t, :, :, :].rearrange("p h g o -> p (h g o)"),
                                     ALU.add).then_inc(bank_drained[t % 2], 1)
                for e in weight_steps(t - 1):
                    dve.wait_ge(w1h_ready, e + 1)
                    cols = slice(e * HID, e * HID + HID)
                    V_.scalar_tensor_tensor(out=W1L[:, cols], in0=W1R[:, e % 4, :], scalar=LNG[:, e:e + 1],
                                            in1=W1H[:, cols].bitcast(F32), op0=ALU.mult,
                                            op1=ALU.subtract).then_inc(w1l_ready, 1)
                j, r = divmod(t - 6, 4)
                if r == 0 and 0 <= j < NG:
                    q0 = (4 * j) % 8
                    dve.wait_ge(*drained("o", 4 * j + 3))
                    sums = OR[:, q0:q0 + 4, :, :, HD].rearrange("p q h w -> p q (h w)")
                    step(V_.scalar_tensor_tensor(out=VA[:, :, :, :].rearrange("p q h w -> p q (h w)"), in0=sums,
                                                 scalar=-1.0 / WT, in1=sums, op0=ALU.mult, op1=ALU.mult))
                    if j >= 1:
                        dve.wait_ge(rsc_ready, j)
                    dve.wait_ge(*filled("st", j))
                    ss = PS[5][:, :].rearrange("p (h q r) -> p q h r", h=4, q=4)[:, :, :, 0:2]
                    V_.tensor_tensor(VB[:, :, :, :], ss, VA[:, :, :, :], ALU.add).then_inc(bank_drained[5], 1)
                j, r = divmod(t - 9, 4)
                if r == 0 and 0 <= j < NG:
                    q0 = (4 * j) % 8
                    dve.wait_ge(rsc_ready, j + 1)
                    if j >= 1:
                        dve.wait_ge(*filled("on", j - 1, 0))
                        dve.wait_ge(*filled("on", j - 1, 1))
                    for q in range(4):
                        V_.tensor_tensor(ON[:, q, :, :, :].rearrange("p w h d -> p h w d"),
                                         OR[:, q0 + q, :, :, 0:HD],
                                         RSC[:, q, :, :].unsqueeze(3).to_broadcast([P, 4, 2, HD]),
                                         ALU.mult).then_inc(on_ready, 1)
                j, r = divmod(t - 12, 4)
                if r == 0 and 0 <= j < NG:
                    x1 = XR[:, 4 * j:4 * j + 4, :]
                    dve.wait_ge(*filled("y", j))
                    V_.tensor_tensor(x1, PS[7][:, 0:256].rearrange("p (q c) -> p q c", q=4), x1,
                                     ALU.add).then_inc(bank_drained[7], 1)
                    dve.wait_ge(*drained("y", j))
                    moments(x1, j).then_inc(mv_ready, 1)
                j, r = divmod(t - 13, 4)
                if r == 0 and 0 <= j < NG:
                    if j >= 1:
                        dve.wait_ge(*filled("zt", j - 1))
                        dve.wait_ge(*filled("x2", j - 1))
                    dve.wait_ge(rz_ready, 2 * j + 1)
                    normalise(lambda q: Z[:, q, :], lambda q: XR[:, 4 * j + q, :], lambda q: RZ[:, 0, j, q:q + 1],
                              j).then_inc(z_ready, 1)
                    dve.wait_ge(z_ready, j + 1)
                    dve.wait_ge(rz_ready, 2 * j + 2)
                    V_.tensor_tensor(Z2[:, :, :, :], Z[:, :, :].unsqueeze(2).to_broadcast([P, 4, 2, C]),
                                     RZ[:, 1, j, :].unsqueeze(2).unsqueeze(3).to_broadcast([P, 4, 2, C]),
                                     ALU.mult).then_inc(z2_ready, 1)
                j, r = divmod(t - 15, 4)
                if r == 0 and 0 <= j < NG:
                    dve.wait_ge(*filled("lg", j))
                    V_.tensor_tensor(LG[:, :, :], PS[6][:, 0:32].rearrange("p (q e) -> p q e", q=4),
                                     BRB[:, :].unsqueeze(1).to_broadcast([P, 4, NE]), ALU.add)\
                        .then_inc(bank_drained[6], 1)
                    dve.wait_ge(*drained("lg", j))
                    step(V_.tensor_reduce(M1[:, :], LG[:, :, :], AX.X, ALU.max))
                    V_.tensor_tensor(LG[:, :, :], LG[:, :, :], M1[:, :].unsqueeze(2).to_broadcast([P, 4, NE]),
                                     ALU.subtract).then_inc(lg_ready, 1)
                    dve.wait_ge(lg_ready, j + 1)
                    dve.wait_ge(x2hi_ready, j + 1)
                    lo = X2[C:P, 512 * j:512 * j + 512]
                    V_.tensor_tensor(lo, PS[5][C:P, :], lo.bitcast(F32), ALU.subtract).then_inc(bank_drained[5], 1)
                    other = LG[:, :, :].unsqueeze(2).to_broadcast([P, 4, NE, NE])
                    own = LG[:, :, :].unsqueeze(3).to_broadcast([P, 4, NE, NE])
                    flat = lambda m: m[:, :, :, :].rearrange("p q e f -> p q (e f)")
                    step(V_.tensor_tensor(CG[:, :, :, :], other, own, ALU.subtract))
                    step(V_.scalar_tensor_tensor(out=flat(CE), in0=flat(CG), scalar=0.0,
                                                 in1=TRI[:, :, :].rearrange("p e f -> p (e f)").unsqueeze(1)
                                                 .to_broadcast([P, 4, NE * NE]),
                                                 op0=ALU.is_equal, op1=ALU.mult))
                    step(V_.scalar_tensor_tensor(out=flat(CG), in0=flat(CG), scalar=0.0, in1=flat(CE),
                                                 op0=ALU.is_gt, op1=ALU.add))
                    step(V_.tensor_reduce(PR[:, :, :], CG[:, :, :, :], AX.X, ALU.add))
                    dve.wait_ge(px_ready, j + 1)
                    step(V_.scalar_tensor_tensor(out=PR[:, :, :], in0=PR[:, :, :], scalar=1.5, in1=PX[:, :, :],
                                                 op0=ALU.is_lt, op1=ALU.mult))
                    step(V_.tensor_reduce(M1[:, :], PR[:, :, :], AX.X, ALU.add))
                    step(V_.reciprocal(M2[:, :], M1[:, :]))
                    step(V_.tensor_tensor(PR[:, :, :], PR[:, :, :], M2[:, :].unsqueeze(2).to_broadcast([P, 4, NE]),
                                          ALU.mult))
                    if j >= 1:
                        dve.wait_ge(*filled("gt", j - 1))
                    step(V_.tensor_copy(G3[:, :, 0, :], PR[:, :, :]))
                    step(V_.tensor_tensor(PR[:, :, :], PR[:, :, :], G3[:, :, 0, :], ALU.subtract))
                    step(V_.tensor_copy(G3[:, :, 1, :], PR[:, :, :]))
                    V_.tensor_tensor(G3[:, :, 2, :], PR[:, :, :], G3[:, :, 1, :], ALU.subtract).then_inc(g3_ready, 1)


def kernel(**inputs):
    import numpy as np
    import concourse.bacc as bacc
    from concourse.bass_utils import run_bass_kernel_spmd

    a = {k: np.asarray(v) for k, v in inputs.items()}
    rel = a["L0_conv_intrinsic"].reshape(2, 4, NREL, 1 + 2 * HD)
    arrays = {
        "x": a["x"].reshape(2, 4, WH, 2, 2, WH, C).transpose(4, 2, 5, 0, 1, 3, 6).reshape(P, NPAIR, C),
        "W_prep": a["L0_conv_W_prep"],
        "b_prep": a["L0_conv_b_prep"].reshape(10, P).T,
        "rel": rel[..., 1:].reshape(2, 4, NREL, 2, HD).transpose(1, 4, 3, 0, 2).reshape(P, 2, 2, NREL),
        "rel0": rel[..., 0].reshape(NH, NREL),
        "W_fin": a["L0_conv_W_fin"].reshape(2, P, C).transpose(1, 0, 2),
        "b_fin": a["L0_conv_b_fin"],
        "Wr": a["L0_ffn_Wr"],
        "br": a["L0_ffn_br"],
        "ln_g": a["L0_ffn_ln_g"].T,
        "ln_b": a["L0_ffn_ln_b"].T,
        "W1": a["L0_ffn_W1"].transpose(1, 0, 2),
        "b1": a["L0_ffn_b1"].reshape(2 * NE, P).T,
        "W2": a["L0_ffn_W2"].reshape(2 * NE, P, C).transpose(1, 0, 2),
        "b2": a["L0_ffn_b2"].reshape(4, P).T,
    }
    arrays = {k: np.ascontiguousarray(v) for k, v in arrays.items()}
    nc = bacc.Bacc("TRN2", target_bir_lowering=False, num_devices=1)
    args = [nc.dram_tensor(f"in_{k}", v.shape, mybir.dt.from_np(v.dtype), kind="ExternalInput").ap()
            for k, v in arrays.items()]
    out = nc.dram_tensor("out", (P, NPAIR, C), F32, kind="ExternalOutput").ap()
    metaformer_kernel(nc, *args, out)
    r = run_bass_kernel_spmd(nc, [{f"in_{k}": v for k, v in arrays.items()}], core_ids=[0])
    y = np.asarray(r.results[0]["out"]).reshape(2, WH, WH, 2, 4, 2, C)
    return np.ascontiguousarray(y.transpose(3, 4, 1, 5, 0, 2, 6).reshape(2, 32, 32, C))
```

```python
from contextlib import ExitStack

import concourse.bass as bass
from concourse import mybir

F32 = mybir.dt.float32
F32R = mybir.dt.float32r
I32 = mybir.dt.int32
BF16 = mybir.dt.bfloat16
ALU = mybir.AluOpType
ACT = mybir.ActivationFunctionType
AX = mybir.AxisListType

P = 128
C = 64
NH, HD = 8, 32
WH = 8
WT = WH * WH
NW = 32
NPAIR = NW // 2
NG = NPAIR // 4
TOK = NW * WT
SIDE = 2 * WH - 1
NREL = SIDE * SIDE
NE, HID = 8, 256
EPS_C, EPS_T, EPS_S = 1e-6, 1e-5, 1e-5
QN, Q, K_, KM, V = range(5)
LAG = 16
KINDS = [QN, QN, KM, KM, Q, Q]


def key_tile(c, i):
    g, s = divmod(i - 4, 2)
    return g, 2 * (c - 2) + s


def stage_b():
    order = []
    for c in range(4):
        held = 6 if c == 3 else 8
        for tile, numbers in ((True, range(2)), (False, range(4)), (True, range(2, 6)), (False, range(4, held)),
                              (True, range(6, 8)), (False, range(held, 8))):
            order += [(tile, c, i) for i in numbers]
    return order


def make_plan():
    plan = [(("b1",), 3, 1)] + [(("xt", j), (0, 1, 2, 7)[j], 1) for j in range(NG)]

    def prep(c, n):
        return [(("bd", c, n), 4 + n, 1 if c else 2)]

    for n in (0, 2, 1, 3):
        plan += prep(0, n)
    for tile, c, i in stage_b():
        if tile:
            plan += [(("t", 8 * c + i), i % 4, 2 if c < 2 else 1)]
        elif c == 0:
            plan += prep(1 + i // 4, i % 4)
        elif i < 4:
            plan += prep(c + 2, i)
        elif c == 1:
            plan += [(("xc", i - 4), i, 1)]
        else:
            plan += [(("k",) + key_tile(c, i), i, 1)]
    for step in range(LAG + NG * 4 + 2):
        plan += [(u, b, r) for u, b, r in pe_steps(step)]
    return plan


def pe_steps(t):
    s = []
    if t < NPAIR:
        if t == 0:
            s.append((("v", 0), 6, 1))
        s.append((("score", t), t % 2, 1))
        if t + 1 < NPAIR:
            s.append((("v", t + 1), 6, 1))
    if 1 <= t <= NPAIR:
        s.append((("o", t - 1), 2 + (t - 1) % 2, 1))
    if 2 <= t <= NPAIR + 1 and (t - 2) % 4 == 3:
        s.append((("ss", (t - 2) // 4), 4, 1))
    elif 2 <= t <= NPAIR + 1:
        s.append((("ss part", t - 2), 4, 0))

    def late(lag, *uses):
        j, r = divmod(t - lag, 4)
        return [((use[0], j) + use[1:], bank, 1) for use, bank in uses] if r == 0 and 0 <= j < NG else []

    if t < LAG:
        s += late(6, (("st",), 5)) + late(10, (("on", 0), 7), (("on", 1), 5))
    s += late(15, (("lg",), 6)) + late(11, (("y",), 7))
    u = t - LAG
    if 0 <= u < 4 * NG:
        s += [(("h", 4 * u), (4 * u) % 3, 1), (("h", 4 * u + 1), (4 * u + 1) % 3, 1)]
    if t >= LAG:
        s += late(6, (("st",), 5)) + late(10, (("on", 0), 7))
    s += late(17, (("gt",), 6))
    if 1 <= u <= 4 * NG:
        s.append((("e", u - 1), 3 + (u - 1) % 2, 1))
    if t >= LAG:
        s += late(10, (("on", 1), 5))
    s += late(14, (("x2",), 6))
    if 0 <= u < 4 * NG:
        s += [(("h", 4 * u + 2), (4 * u + 2) % 3, 1), (("h", 4 * u + 3), (4 * u + 3) % 3, 1)]
    if 1 <= u <= 4 * NG:
        s.append((("gb", u - 1), 5, 1))
    if 0 <= u < 4 * NG:
        s.append((("e part", u), 3 + u % 2, 0))
    return s + late(LAG + 5, (("out",), 6))


def metaformer_kernel(nc, x, W_prep, b_prep, rel, rel0, W_fin, b_fin, Wr, br, ln_g, ln_b, W1, b1,
                      W2, b2, out):
    before, at_fill, at_drain = {}, {}, {}
    fills, drains = [0] * 8, [0] * 8
    open_part = {}
    for use, bank, readers in make_plan():
        if readers == 0:
            if bank not in open_part:
                open_part[bank] = drains[bank]
            before[use] = (bank, open_part[bank])
            continue
        before[use] = (bank, open_part.pop(bank, drains[bank]))
        fills[bank] += 1
        drains[bank] += readers
        at_fill[use], at_drain[use] = (bank, fills[bank]), (bank, drains[bank])

    with ExitStack() as ctx:
        sem = lambda name: ctx.enter_context(nc.semaphore(name))
        bank_filled = [sem(f"bank{b}_filled") for b in range(8)]
        bank_drained = [sem(f"bank{b}_drained") for b in range(8)]
        PS = [ctx.enter_context(nc.psum_tensor(f"PS{b}", [P, 512], F32)) for b in range(8)]

        def filled(*use):
            return bank_filled[at_fill[use][0]], at_fill[use][1]

        def drained(*use):
            return bank_drained[at_drain[use][0]], at_drain[use][1]

        base = 16640
        arena = ctx.enter_context(nc.sbuf_tensor("arena", [P, (229344 - base - 512) // 4], F32))
        cursor = [base]

        def sb(name, shape, dt=F32, at=None):
            size = 2 if dt == BF16 else 4
            for n in shape[1:]:
                size *= n
            size = -(-size // 32) * 32
            where = at if at is not None else cursor
            t = nc.alloc_sbuf_tensor_at(name, shape, dt, offset=where[0])
            where[0] += size
            return t

        XR = sb("XR", [P, NPAIR, C])
        W2s = sb("W2s", [P, 16, C])
        KT = sb("KT", [P, 2, TOK])
        XC = sb("XC", [P, TOK], F32R)
        WVH = sb("WVH", [P, 256], F32R)
        WVL = sb("WVL", [P, 256], F32R)
        WF = sb("WF", [P, 2, C])
        IDN = sb("IDN", [P, P])
        IDB = sb("IDB", [P, P], BF16)
        ONES2 = sb("ONES2", [P, 32])
        SEL = sb("SEL", [24, 4, P], BF16)
        TRI = sb("TRI", [P, NE, NE], BF16)
        BP = sb("BP", [P, 10])
        B1 = sb("B1", [P, 16])
        B1P = sb("B1P", [P, 16])
        B2 = sb("B2", [P, 4])
        LNG = sb("LNG", [P, NE])
        BRB = sb("BRB", [P, NE])
        WRs = sb("WRs", [P, NE])
        WRR = sb("WRR", [P, 2, NE], F32R)
        MV = sb("MV", [P, NPAIR, 2])
        RZ = sb("RZ", [P, 3, NG, 4])
        NHALF = sb("NHALF", [P, 32])
        BNS = sb("BNS", [P, 4, 6])
        tn_at = [cursor[0]]
        TN = sb("TN", [P, NPAIR, 4, 2, WT])
        tm_at = [cursor[0]]
        TM = sb("TM", [P, P, WT])
        bd_at = [[cursor[0]], [cursor[0] + 32768]]
        BD = [sb(f"BD{n}", [P, 2, 4, 1024]) for n in range(2)]
        region = cursor[0]

        XN = sb("XN", [P, NPAIR, 2, C], at=tm_at)
        CEN = sb("CEN", [P, P], at=tm_at)
        LNB = sb("LNB", [C, NE], at=tm_at)
        BFB = sb("BFB", [P, C], at=tm_at)
        RB = sb("RB", [NH, NREL], at=tm_at)
        EB = sb("EB", [NH, WH, SIDE, WH], at=tm_at)
        VE = sb("VE", [P, NPAIR], at=tm_at)
        RS = sb("RS", [P, NPAIR], at=tm_at)
        RA = sb("RA", [P, NPAIR], at=tm_at)
        BNX = sb("BNX", [P, NPAIR, 6], at=tm_at)
        WARM = sb("WARM", [P, 1], at=tm_at)
        NB = sb("NB", [P, NPAIR], at=tm_at)
        WS = sb("WS", [P, 1280], at=tm_at)
        REL = sb("REL", [P, 2, 2, NREL], at=tm_at)
        PN = sb("PN", [P, 2, WH, SIDE, WH], at=tm_at)
        W1E = sb("W1E", [C, NE * HID], at=tn_at)
        r_at = [region]
        WHI = sb("WHI", [P, 1024], F32R, at=r_at)
        WLO = sb("WLO", [P, 1024], F32R, at=r_at)
        XS = sb("XS", [P, NW, WT], F32R, at=r_at)
        ab_at = [r_at[0]]
        PM = sb("PM", [P, 2, WH, SIDE, WH], at=r_at)
        BI = sb("BI", [P, 4, WT], at=r_at)
        stg1 = r_at[0] + 4 * 2048
        STG = [sb(f"STG{n}", [P, 2, 1024], at=r_at) for n in range(2)]
        late = [region]
        OR = sb("OR", [P, 8, 4, 2, HD + 1], at=late)
        ON = sb("ON", [P, 4, 2, 4, HD], at=late)
        ONT = sb("ONT", [P, 4, 2, P], at=late)
        VA = sb("VA", [P, 4, 4, 2], at=late)
        VB = sb("VB", [P, 4, 4, 2], at=late)
        RSC = sb("RSC", [P, 4, 4, 2], at=late)
        PX = sb("PX", [P, 4, NE], at=late)
        M1 = sb("M1", [P, 4], at=late)
        AR = sb("AR", [P, 4, NE], at=late)
        G3 = sb("G3", [P, 4, 3, NE], BF16, at=late)
        ab_at[0] = max(ab_at[0], late[0])
        SR = [sb(f"SR{n}", [P, 512], at=ab_at) for n in range(2)]
        SQ = [sb(f"SQ{n}", [P, 512], at=ab_at) for n in range(2)]
        BV = [sb(f"BV{n}", [P, NH, 2, HD + 1], at=ab_at) for n in range(3)]
        assert ab_at[0] <= stg1, (ab_at, stg1)
        SR.append(sb("SR2", [P, 512], at=ab_at))
        rest = [ab_at[0]]
        SSB = sb("SSB", [P, 512], at=rest)
        LG = sb("LG", [P, 4, NE], at=rest)
        PR = sb("PR", [P, 4, NE], at=rest)
        Z = sb("Z", [P, 4, C], at=rest)
        Z2 = sb("Z2", [P, 4, 2, C], at=rest)
        CG = sb("CG", [P, 4, NE, NE], at=rest)
        CE = sb("CE", [P, 4, NE, NE], BF16, at=rest)
        assert rest[0] <= 229344, rest
        W1H = sb("W1H", [P, NE * HID], F32R, at=bd_at[0])
        W1L = sb("W1L", [P, NE * HID], F32R, at=bd_at[0])
        X2 = sb("X2", [P, TOK], F32R, at=bd_at[0])
        W1R = sb("W1R", [P, 4, HID], at=bd_at[0])
        GT = sb("GT", [24, TOK], BF16, at=bd_at[0])
        HR = [sb(f"HR{n}", [P, 512], at=bd_at[1]) for n in range(4)]
        GB = [sb(f"GB{n}", [P, 512], at=bd_at[1]) for n in range(2)]
        AC = [sb(f"AC{n}", [P, 512], at=bd_at[1]) for n in range(2)]
        GM = sb("GM", [P, 512], at=bd_at[1])
        scratch = nc.dram_tensor("bias_rows", [NH, WH, SIDE * WH], F32).ap()

        x_in = [sem(f"x_in{j}") for j in range(NG)]
        wprep_in = sem("wprep_in")
        w1e_in = sem("w1e_in")
        lnb_in = sem("lnb_in")
        b1_in = sem("b1_in")
        reln_in = sem("reln_in")
        relm_in = sem("relm_in")
        rel0_in = sem("rel0_in")
        small_in = sem("small_in")
        bias_out = sem("bias_out")
        bias_in = sem("bias_in")
        w1r_in = sem("w1r_in")
        result_out = sem("result_out")
        dve_step = sem("dve_step")
        pool_step = sem("pool_step")
        consts_ready = sem("consts_ready")
        bd_zeroed = sem("bd_zeroed")
        bv_zeroed = sem("bv_zeroed")
        pm_ready = sem("pm_ready")
        pn_ready = sem("pn_ready")
        bias_rows = sem("bias_rows_ready")
        whi_ready = sem("whi_ready")
        wlo_ready = sem("wlo_ready")
        mv_ready = sem("mv_ready")
        rsc_ready = sem("rsc_ready")
        rz_ready = sem("rz_ready")
        wvh_ready = sem("wvh_ready")
        wvl_ready = sem("wvl_ready")
        xchi_ready = sem("xchi_ready")
        bd_in = [sem(f"bd_in{n}") for n in range(2)]
        half_zeroed = sem("half_zeroed")
        first_spread = sem("first_spread")
        rx_ready = sem("rx_ready")
        xn_ready = sem("xn_ready")
        xn2_ready = sem("xn2_ready")
        xhi_ready = sem("xhi_ready")
        sq_ready = sem("sq_ready")
        on_ready = sem("on_ready")
        wrh_ready = sem("wrh_ready")
        wrr_ready = sem("wrr_ready")
        z2_ready = sem("z2_ready")
        x2hi_ready = sem("x2hi_ready")
        arg_ready = sem("arg_ready")
        tanh_ready = sem("tanh_ready")
        g3_ready = sem("g3_ready")
        w1h_ready = sem("w1h_ready")
        w1l_ready = sem("w1l_ready")
        down_done = sem("down_done")
        gate_done = sem("gate_done")
        sq_used = sem("sq_used")
        xb_ready = sem("xb_ready")

        def moved(c):
            return bd_in[c % 2], 4 * 16 * ((c + 1) // 2)

        block = ctx.enter_context(nc.Block())

        @block.sync
        def _(sp):
            for j in range(NG):
                sp.dma_start(XR[:, 4 * j:4 * j + 4, :], x[:, 4 * j:4 * j + 4, :]).then_inc(x_in[j], 16)
            sp.dma_start(W1E[:, :].rearrange("p (e h) -> p e h", e=NE), W1).then_inc(w1e_in, 16)
            sp.dma_start(REL[:, 0, :, :], rel[:, 0, :, :]).then_inc(reln_in, 16)
            sp.dma_start(WS[0:C, :], W_prep).then_inc(wprep_in, 16)
            sp.dma_start(WS[C:P, :], W_prep).then_inc(wprep_in, 16)
            sp.dma_start(B1[:, :], b1).then_inc(b1_in, 16)
            sp.dma_start(REL[:, 1, :, :], rel[:, 1, :, :]).then_inc(relm_in, 16)
            for dst, src in ((BP[:, :], b_prep),
                             (B2[:, :], b2), (LNG[0:C, :], ln_g), (LNG[C:P, :], ln_g),
                             (BFB[:, :], b_fin.partition_broadcast(P)),
                             (BRB[:, :], br.partition_broadcast(P)), (WRs[0:C, :], Wr), (WRs[C:P, :], Wr),
                             (WF[:, :, :], W_fin), (W2s[:, :, :], W2)):
                sp.dma_start(dst, src).then_inc(small_in, 16)
            for c in range(1, 6):
                for n in range(4):
                    sp.wait_ge(*drained("bd", c, n))
                if c == 1:
                    sp.wait_ge(bd_zeroed, 2)
                else:
                    sp.wait_ge(*filled("t", 8 * (c - 2) + 7))
                for h in range(4):
                    r = slice(HD * h, HD * h + HD)
                    sp.dma_start(BD[c % 2][r, :, h, :], STG[c % 2][r, :, :]).then_inc(bd_in[c % 2], 16)
                if c == 1:
                    sp.wait_ge(bias_rows, 1)
                    sp.dma_start(scratch, EB[:, :, :, :].rearrange("h j r c -> h j (r c)")).then_inc(bias_out, 16)
                    sp.wait_ge(bias_out, 16)
                    for g in range(2):
                        for oy in range(WH):
                            lo = (WH - 1 - oy) * WH
                            src = scratch[4 * g:4 * g + 4, :, lo:lo + WT].rearrange("h j i -> j h i")
                            r0 = g * C + oy * WH
                            sp.dma_start(BI[r0:r0 + WH, :, :], src).then_inc(bias_in, 16)
            sp.wait_ge(*filled("score", NPAIR // 2 - 1))
            for half in range(2):
                if half:
                    sp.wait_ge(w1l_ready, 4)
                for d in range(2):
                    sp.dma_start(W1R[d * C:d * C + C, :, :], W1[:, 4 * half:4 * half + 4, :]).then_inc(w1r_in, 16)
            for j in range(NG):
                sp.wait_ge(*drained("out", j))
                sp.dma_start(out[:, 4 * j:4 * j + 4, :], XR[:, 4 * j:4 * j + 4, :]).then_inc(result_out, 16)
            sp.wait_ge(result_out, 16 * NG)

        N_SMALL = 10
        FIRST = 8
        NDVE = 3

        @block.gpsimd
        def _(pool):
            n = [0]

            def step(ins):
                n[0] += 1
                ins.then_inc(pool_step, 1)
                pool.wait_ge(pool_step, n[0])

            pool.dma_start(LNB[:, :], ln_b).then_inc(lnb_in, 16)
            pool.dma_start(RB[:, :], rel0).then_inc(rel0_in, 16)
            step(pool.memset(IDN[:, :], 0.0))
            pool.affine_select(out=IDN[:, :], in_=IDN[:, :], compare_op=ALU.not_equal, fill=1.0, base=0,
                               pattern=[[-1, P]], channel_multiplier=1).then_inc(consts_ready, 1)
            step(pool.memset(NHALF[:, :], -0.5))
            step(pool.memset(BD[0][:, 0, 2:4, :], 0.0))
            step(pool.memset(BD[0][:, 1, 0:2, :], 0.0))
            pool.memset(BD[0][:, 1, 2:4, :], 0.0).then_inc(bd_zeroed, 1)
            pool.wait_ge(bd_zeroed, 1)
            pool.wait_ge(whi_ready, 1)
            nc.gpsimd.tensor_tensor(WLO[:, :], WS[:, 0:V * 256], WHI[:, :].bitcast(F32),
                                    ALU.subtract).then_inc(wlo_ready, 1)
            pool.wait_ge(wlo_ready, 1)
            pool.memset(BD[1][:, :, :, :], 0.0).then_inc(bd_zeroed, 1)
            step(pool.memset(CEN[:, :], 0.0))
            step(pool.memset(CEN[0:C, 0:C], -1.0 / WT))
            step(pool.memset(CEN[C:P, C:P], -1.0 / WT))
            pool.wait_ge(consts_ready, 1)
            pool.tensor_tensor(CEN[:, :], CEN[:, :], IDN[:, :], ALU.add).then_inc(consts_ready, 1)
            pool.wait_ge(relm_in, 16)
            for ij in range(WH):
                src = REL[:, 1, :, :].rearrange("p g (r c) -> p g r c", c=SIDE)
                pool.tensor_copy(PM[:, :, ij, :, :], src[:, :, :, WH - 1 - ij:2 * WH - 1 - ij]).then_inc(pm_ready, 1)
            pool.wait_ge(small_in, 16 * N_SMALL)
            pool.wait_ge(xn_ready, NDVE)
            pool.wait_ge(xn2_ready, NG - NDVE)
            nc.gpsimd.tensor_tensor(XR[:, :, :], XR[:, :, :], BFB[:, :].unsqueeze(1).to_broadcast([P, NPAIR, C]),
                                    ALU.add).then_inc(xb_ready, 1)
            pool.wait_ge(xb_ready, 1)
            step(pool.memset(ONES2[:, :], 0.0))
            step(pool.memset(ONES2[0:C, 0:1], 1.0))
            step(pool.memset(ONES2[C:P, 1:2], 1.0))
            step(pool.memset(SEL[:, :, :], 0.0))
            sel = SEL[:, :, :].rearrange("k p (d c) -> k p d c", d=2)
            for part in range(3):
                step(pool.affine_select(out=sel, in_=sel, compare_op=ALU.not_equal, fill=1.0, base=-NE * part,
                                        pattern=[[-2, 4], [-1, 2], [0, C]], channel_multiplier=1))
            step(pool.memset(TRI[:, :, :], 1.0))
            step(pool.affine_select(out=TRI[:, :, :], in_=TRI[:, :, :], compare_op=ALU.is_gt, fill=0.0, base=0,
                                    pattern=[[1, NE], [-1, NE]], channel_multiplier=0))
            pool.tensor_copy(IDB[:, :], IDN[:, :]).then_inc(consts_ready, 1)
            pool.wait_ge(*filled("t", 31))
            pool.wait_ge(*moved(4))
            for m, v in enumerate(BV):
                step(pool.memset(v[:, :, :, :], 0.0))
                step(pool.memset(v[0:C, :, 0, HD:HD + 1], 1.0))
                pool.memset(v[C:P, :, 1, HD:HD + 1], 1.0).then_inc(bv_zeroed, 1)
                pool.wait_ge(bv_zeroed, m + 1)
            G = nc.gpsimd
            for t in range(NPAIR + 12):
                j, r = divmod(t - 6, 4)
                if r == 0 and 0 <= j < NG:
                    pool.wait_ge(*drained("st", j))
                    vb = VB[:, :, :, :].rearrange("p q h g -> p (q h g)")
                    step(G.tensor_scalar(vb, vb, 0.0, 1.0 / (WT - 1), ALU.max, ALU.mult))
                    step(G.tensor_scalar(vb, vb, EPS_S, None, ALU.add))
                    if j >= 1:
                        pool.wait_ge(on_ready, 4 * j)
                    G.tensor_tensor(RSC[:, :, :, :].rearrange("p q h g -> p (q h g)"), vb, NHALF[:, :],
                                    ALU.pow).then_inc(rsc_ready, 1)
                j, r = divmod(t - 12, 4)
                if r == 0 and 0 <= j < NG:
                    pool.wait_ge(mv_ready, j + 1)
                    pool.wait_ge(rsc_ready, min(j + 2, NG))
                    v, r1, r2 = MV[:, 4 * j:4 * j + 4, 1], RZ[:, 0, j, :], RZ[:, 1, j, :]
                    work = RZ[:, 2, j, :]
                    step(G.tensor_scalar(work, v, EPS_T, None, ALU.add))
                    G.tensor_tensor(r1, work, NHALF[:, 0:4], ALU.pow).then_inc(rz_ready, 1)
                    pool.wait_ge(rz_ready, 3 * j + 1)
                    step(G.tensor_tensor(work, r1, r1, ALU.mult))
                    step(G.tensor_tensor(work, work, v, ALU.mult))
                    step(G.tensor_scalar(work, work, EPS_T, None, ALU.add))
                    G.tensor_tensor(r2, work, NHALF[:, 0:4], ALU.pow).then_inc(rz_ready, 1)
                    pool.wait_ge(rz_ready, 3 * j + 2)
                    G.tensor_tensor(work, work, r2, ALU.mult).then_inc(rz_ready, 1)
                    pool.wait_ge(rz_ready, 3 * j + 3)

        @block.tensor
        def _(pe):
            def begin(*use):
                bank, count = before[use]
                if count:
                    pe.wait_ge(bank_drained[bank], count)
                return PS[bank]

            def end(ins, *use):
                ins.then_inc(bank_filled[at_fill[use][0]], 1)

            def shift_bias(experts):
                for e in experts:
                    for c in range(2):
                        m = nc.tensor.matmul(PS[3][:, 2 * e + c:2 * e + c + 1],
                                             W1E[:, e * HID + c * P:e * HID + c * P + P],
                                             LNB[:, e:e + 1], start=True, stop=True)
                return m

            pe.wait_ge(w1e_in, 16)
            pe.wait_ge(lnb_in, 16)
            shift_bias(range(5))
            pe.wait_ge(consts_ready, 1)
            for j in range(NG):
                if j < NDVE:
                    pe.wait_ge(xn_ready, j + 1)
                else:
                    pe.wait_ge(xn2_ready, j - NDVE + 1)
                ps = begin("xt", j)
                for n in range(4):
                    m = nc.tensor.transpose(ps[:, n * P:n * P + P],
                                            XN[:, 4 * j + n, :, :].rearrange("p d c -> p (d c)"), IDN[:, :])
                end(m, "xt", j)

            def centred(j):
                if j == 0:
                    pe.wait_ge(consts_ready, 2)
                ps = begin("xc", j)
                for n in range(4):
                    m = nc.tensor.matmul(ps[:, n * P:n * P + P],
                                         XN[:, 4 * j + n, :, :].rearrange("p d c -> p (d c)"), CEN[:, :],
                                         start=True, stop=True)
                end(m, "xc", j)

            def keys(g, s):
                ps = begin("k", g, s)
                end(project(ps, K_, g, XS[:, 8 * s:8 * s + 8, :]), "k", g, s)

            def project(ps, kind, g, moving):
                col = kind * 256 + g * P
                nc.tensor.matmul(ps[:, :], WHI[:, col:col + P], moving, start=True, stop=False)
                return nc.tensor.matmul(ps[:, :], WLO[:, col:col + P], moving, start=False, stop=True)

            pe.wait_ge(whi_ready, 1)
            pe.wait_ge(wlo_ready, 1)
            def prep(c, n):
                g, s = divmod(n, 2)
                half = c % 2
                if KINDS[c] == Q:
                    w0 = 16 * half + 8 * s
                    moving = XS[:, w0:w0 + 8, :]
                else:
                    moving = XS[:, 16 * s:16 * s + 16, 32 * half:32 * half + 32]
                ps = begin("bd", c, n)
                end(project(ps, KINDS[c], g, moving), "bd", c, n)

            def pattern(tile):
                c, i = divmod(tile, 8)
                table = PN if c < 2 else PM
                slot = BD[c % 2]
                if tile == 0:
                    pe.wait_ge(first_spread, 2)
                elif tile == FIRST // 4:
                    for n in range(4):
                        pe.wait_ge(*drained("bd", 0, n))
                elif i == 0:
                    pe.wait_ge(*moved(c))
                ps = begin("t", tile)
                for u in range(4):
                    local = 4 * i + u
                    fy, fx = divmod(32 * (c % 2) + local, WH)
                    for g in range(2):
                        rows = table[:, g, fx, WH - 1 - fy:2 * WH - 1 - fy, :].rearrange("p a b -> p (a b)")
                        moving = slot[:, g, :, 32 * local:32 * local + 32]
                        m = nc.tensor.matmul(ps[g * C:g * C + C, u * P:u * P + P], rows, moving,
                                             start=True, stop=True)
                end(m, "t", tile)

            for n in (0, 2, 1, 3):
                if n < 2:
                    pe.wait_ge(*drained("xt", 2 * n))
                    pe.wait_ge(*drained("xt", 2 * n + 1))
                prep(0, n)
            end(shift_bias(range(5, NE)), "b1")
            pe.wait_ge(pn_ready, 1)
            for tile, c, i in stage_b():
                if tile:
                    if (c, i) == (2, 0):
                        pe.wait_ge(pm_ready, WH)
                    pattern(8 * c + i)
                elif c == 0:
                    prep(1 + i // 4, i % 4)
                elif i < 4:
                    prep(c + 2, i)
                elif c == 1:
                    centred(i - 4)
                else:
                    keys(*key_tile(c, i))

            def values(t):
                ps = begin("v", t)
                nc.tensor.matmul(ps[:, 0:256], XC[:, t * P:t * P + P], WVH[:, :], start=True, stop=False)
                end(nc.tensor.matmul(ps[:, 0:256], XC[:, t * P:t * P + P], WVL[:, :], start=False, stop=True), "v", t)

            def score(t):
                if t == 0:
                    pe.wait_ge(*drained("t", 31))
                    pe.wait_ge(*moved(4))
                if t % 4 == 0:
                    for g in range(2):
                        pe.wait_ge(*drained("k", g, t // 4))
                if t == NPAIR // 2:
                    pe.wait_ge(*moved(5))
                slot = BD[t // (NPAIR // 2)]
                ps = begin("score", t)
                for h in range(4):
                    pair = TM[:, h * NW + 2 * t:h * NW + 2 * t + 2, :].rearrange("p w i -> p (w i)")
                    nc.tensor.matmul(ps[:, h * P:h * P + P], pair, IDN[:, :], start=(h == 0), stop=False,
                                     is_transpose=True, skip_group_check=True)
                for g in range(2):
                    for w in range(2):
                        lo = (2 * t + w) * WT
                        lq = lo % 1024
                        dst = ps[w * C:w * C + C, :].rearrange("p (h g o) -> p h g o", h=4, g=2)[:, :, g, :]
                        m = nc.tensor.matmul(dst, KT[:, g, lo:lo + WT], slot[:, g, :, lq:lq + WT],
                                             start=False, stop=True, skip_group_check=True)
                end(m, "score", t)

            def weighted(t):
                pe.wait_ge(*drained("score", t))
                pe.wait_ge(*drained("v", t))
                ps = begin("o", t)
                for h in range(4):
                    for g in range(2):
                        dst = ps[g * C:g * C + C, h * 66:h * 66 + 66]
                        m = nc.tensor.matmul(dst, SR[t % 3][:, (2 * h + g) * C:(2 * h + g) * C + C],
                                             BV[t % 3][:, 4 * g + h, :, :].rearrange("p w d -> p (w d)"),
                                             start=True, stop=True)
                end(m, "o", t)

            def squares(t):
                q = t % 4
                pe.wait_ge(sq_ready, t + 1)
                last = q == 3
                ps = begin("ss", t // 4) if last else begin("ss part", t)
                m = nc.tensor.matmul(ps[32 * q:32 * q + 32, :], ONES2[:, :], SQ[t % 2][:, :], start=True, stop=True)
                m.then_inc(bank_filled[4] if last else sq_used, 1)

            def hidden(n):
                u, r = divmod(n, 4)
                j, ep = divmod(u, 4)
                c, d = divmod(r, 2)
                col = (2 * ep + d) * HID + c * P
                ps = begin("h", n)
                nc.tensor.matmul(ps[:, :], W1H[:, col:col + P], X2[:, j * 512:j * 512 + 512], start=True, stop=False)
                end(nc.tensor.matmul(ps[:, :], W1L[:, col:col + P], X2[:, j * 512:j * 512 + 512],
                                     start=False, stop=True), "h", n)

            def down(u, c):
                ep = u % 4
                pe.wait_ge(*drained("h", 4 * u + 2 * c))
                pe.wait_ge(*drained("h", 4 * u + 2 * c + 1))
                ps = begin("e part", u) if c == 0 else PS[before[("e", u)][0]]
                for d in range(2):
                    m = nc.tensor.matmul(ps[d * C:d * C + C, :], W2s[:, 2 * (2 * ep + d) + c, :],
                                         HR[(2 * c + d) % 4][:, :], start=(c == 0), stop=(c == 1),
                                         skip_group_check=True)
                m.then_inc(down_done if c == 0 else bank_filled[before[("e", u)][0]], 1)

            for t in range(LAG + 4 * NG + 2):
                for use, _, _ in pe_steps(t):
                    kind, a = use[0], use[1]
                    if kind == "v":
                        if a == 0:
                            pe.wait_ge(wvh_ready, 1)
                            pe.wait_ge(wvl_ready, 1)
                            pe.wait_ge(*drained("xc", NG - 1))
                        values(a)
                    elif kind == "score":
                        score(a)
                    elif kind == "o":
                        if a < 3:
                            pe.wait_ge(bv_zeroed, a + 1)
                        weighted(a)
                    elif kind == "ss part":
                        if a == 0:
                            pe.wait_ge(consts_ready, 3)
                        squares(a)
                    elif kind == "ss":
                        squares(4 * a + 3)
                    elif kind == "st":
                        pe.wait_ge(*drained("ss", a))
                        ps = begin("st", a)
                        for h in range(4):
                            m = nc.tensor.transpose(ps[:, h * P:h * P + P], SSB[:, h * P:h * P + P], IDN[:, :])
                        end(m, "st", a)
                    elif kind == "on":
                        half = use[2]
                        pe.wait_ge(on_ready, 4 * a + 2 * half + 2)
                        ps = begin("on", a, half)
                        for q in range(2):
                            for w in range(2):
                                m = nc.tensor.transpose(ps[:, (2 * q + w) * P:(2 * q + w) * P + P],
                                                        ON[:, 2 * half + q, w, :, :].rearrange("p h d -> p (h d)"),
                                                        IDN[:, :])
                        end(m, "on", a, half)
                    elif kind == "y":
                        if a == 0:
                            pe.wait_ge(small_in, 16 * N_SMALL)
                        pe.wait_ge(*drained("on", a, 1))
                        ps = begin("y", a)
                        for q in range(4):
                            for g in range(2):
                                m = nc.tensor.matmul(ps[:, q * C:q * C + C], ONT[:, q, g, :], WF[:, g, :],
                                                     start=(g == 0), stop=(g == 1))
                        end(m, "y", a)
                    elif kind == "lg":
                        if a == 0:
                            pe.wait_ge(wrr_ready, 1)
                        pe.wait_ge(*drained("x2", a))
                        ps = begin("lg", a)
                        for q in range(4):
                            lo = (4 * a + q) * P
                            m = nc.tensor.matmul(ps[:, 2 * q * NE:2 * (q + 1) * NE], X2[:, lo:lo + P],
                                                 WRR[:, :, :].rearrange("p k e -> p (k e)"), start=True, stop=True)
                        end(m, "lg", a)
                    elif kind == "x2":
                        pe.wait_ge(z2_ready, a + 1)
                        ps = begin("x2", a)
                        for q in range(4):
                            m = nc.tensor.transpose(ps[:, q * P:q * P + P],
                                                    Z2[:, q, :, :].rearrange("p d c -> p (d c)"), IDN[:, :])
                        end(m, "x2", a)
                    elif kind == "gt":
                        pe.wait_ge(g3_ready, a + 1)
                        ps = begin("gt", a)
                        half_words = ps[0:24, 0:256].bitcast(BF16)
                        for q in range(4):
                            m = nc.tensor.transpose(half_words[:, q * P:q * P + P],
                                                    G3[:, q, :, :].rearrange("p k e -> p (k e)"), IDB[:, :])
                        end(m, "gt", a)
                    elif kind == "gb":
                        if a % 4 == 0:
                            pe.wait_ge(*drained("gt", a // 4))
                        ps = begin("gb", a)
                        end(nc.tensor.matmul(ps[:, :], SEL[:, a % 4, :], GT[:, (a // 4) * 512:(a // 4) * 512 + 512],
                                             start=True, stop=True), "gb", a)
                    elif kind == "h":
                        if a == 0:
                            pe.wait_ge(w1h_ready, NE)
                            pe.wait_ge(w1l_ready, NE)
                        if a % 16 == 0:
                            pe.wait_ge(*drained("x2", a // 16))
                        hidden(a)
                    elif kind == "e part":
                        down(a, 0)
                    elif kind == "e":
                        down(a, 1)
                    elif kind == "out":
                        last = a == NG - 1
                        pe.wait_ge(gate_done, 3 * a + (2 if last else 3))
                        ps = begin("out", a)
                        for src in [AC[a % 2], GM] if last else [AC[a % 2]]:
                            if src is GM:
                                pe.wait_ge(*drained("e", 4 * NG - 1))
                            for q in range(4):
                                m = nc.tensor.matmul(ps[:, q * P:q * P + P], src[:, q * P:q * P + P], IDN[:, :],
                                                     start=(q == 0 and src is not GM),
                                                     stop=(q == 3 and (not last or src is GM)),
                                                     is_transpose=True, skip_group_check=True)
                        end(m, "out", a)

        def weight_steps(t):
            return {9: (0, 1), 10: (2, 3), 13: (4, 5), 14: (6, 7)}.get(t, ())

        def twice(x):
            return x.unsqueeze(1).to_broadcast([P, 2, C])

        def token_order(c, dst):
            return dst if KINDS[c] == Q else dst.rearrange("p (o w) -> p w o", w=NW)

        def spread_first(engine, add, heads):
            engine.wait_ge(bd_zeroed, 1)
            engine.wait_ge(half_zeroed, 1)
            for part in range(2):
                tokens = slice(FIRST, 32) if part else slice(0, FIRST)
                for n in range(4) if part else (0, 2, 1, 3):
                    g, s = divmod(n, 2)
                    if part == 0:
                        engine.wait_ge(*filled("bd", 0, n))
                    for h in heads:
                        r = slice(HD * h, HD * h + HD)
                        dst = token_order(0, BD[0][r, g, h, :])[:, 16 * s:16 * s + 16, tokens]
                        last = add(dst, PS[4 + n][r, :].rearrange("p (w o) -> p w o", w=16)[:, :, tokens],
                                   BP[r, 2 * KINDS[0] + g:2 * KINDS[0] + g + 1])
                    if part:
                        last.then_inc(bank_drained[4 + n], 1)
                    elif n == 3:
                        last.then_inc(first_spread, 1)

        def stage(engine, add, c, n):
            g, s = divmod(n, 2)
            if c >= 3:
                engine.wait_ge(*moved(c - 2))
            engine.wait_ge(*filled("bd", c, n))
            bias = BP[:, 2 * KINDS[c] + g:2 * KINDS[c] + g + 1]
            if KINDS[c] == Q:
                last = add(STG[c % 2][:, g, 512 * s:512 * s + 512], PS[4 + n][:, :], bias)
            else:
                last = add(token_order(c, STG[c % 2][:, g, :])[:, 16 * s:16 * s + 16, :],
                           PS[4 + n][:, :].rearrange("p (w o) -> p w o", w=16), bias)
            last.then_inc(bank_drained[4 + n], 1)

        def move_tn(engine, copy, tile, g):
            o0 = 4 * tile
            engine.wait_ge(*filled("t", tile))
            for w in range(2):
                src = PS[tile % 4][g * C:g * C + C, :].rearrange("p (o h t w) -> p w o h t", o=4, h=4, w=2)[:, w]
                last = copy(TN[w * C:w * C + C, :, :, g, o0:o0 + 4].rearrange("p t h o -> p o h t"), src)
            last.then_inc(bank_drained[tile % 4], 1)

        @block.scalar
        def _(act):
            A = nc.scalar.activation

            def act_spread(dst, src, bias):
                return A(dst, src, ACT.Identity, bias=bias)

            act.wait_ge(x_in[0], 16)
            A(WARM[:, :], XR[:, 0, 0:1], ACT.Gelu)
            act.wait_ge(reln_in, 16)
            for oj in range(WH):
                src = REL[:, 0, :, ::-1].rearrange("p g (y c) -> p g y c", c=SIDE)
                last = A(PN[:, :, oj, :, :], src[:, :, :, WH - 1 - oj:2 * WH - 1 - oj], ACT.Copy)
            last.then_inc(pn_ready, 1)
            act.wait_ge(wprep_in, 32)
            A(WHI[:, :], WS[:, 0:V * 256], ACT.Copy).then_inc(whi_ready, 1)
            act.wait_ge(rx_ready, 1)
            for j in range(NDVE, NG):
                for n in range(4 * j, 4 * j + 4):
                    last = A(XN[:, n, :, :], twice(XR[:, n, :]), ACT.Identity,
                             scale=RS[:, n:n + 1], bias=NB[:, n:n + 1])
                last.then_inc(xn2_ready, 1)
            for j in range(NG):
                act.wait_ge(*filled("xt", j))
                A(XS[:, 8 * j:8 * j + 8, :].rearrange("p w o -> p (w o)"), PS[before[("xt", j)][0]][:, :],
                  ACT.Copy).then_inc(xhi_ready, 1)
            act.wait_ge(small_in, 16 * N_SMALL)
            spread_first(act, act_spread, range(2))
            A(WVH[:, :], WS[:, V * 256:], ACT.Copy).then_inc(wvh_ready, 1)
            A(WRR[:, 0, :], WRs[:, :], ACT.Copy).then_inc(wrh_ready, 1)
            for tile, c, i in stage_b():
                if tile:
                    if c < 2:
                        move_tn(act, lambda dst, src: A(dst, src, ACT.Copy), 8 * c + i, 0)
                    continue
                if c == 0:
                    if i >= 4 or i % 2 == 0:
                        stage(act, act_spread, 1 + i // 4, i % 4)
                    continue
                if i < 4:
                    stage(act, act_spread, c + 2, i)
                    continue
                b = i
                if c == 1:
                    j = i - 4
                    act.wait_ge(*filled("xc", j))
                    A(XC[:, 512 * j:512 * j + 512], PS[b][:, :], ACT.Copy).then_inc(xchi_ready, 1)
                elif c >= 2:
                    g, s = key_tile(c, i)
                    act.wait_ge(*filled("k", g, s))
                    A(KT[:, g, 512 * s:512 * s + 512], PS[b][:, :], ACT.Identity,
                      bias=BP[:, 2 * K_ + g:2 * K_ + g + 1]).then_inc(bank_drained[b], 1)

            def hidden_act(n):
                u, r = divmod(n, 4)
                ep = u % 4
                c, d = divmod(r, 2)
                col = 2 * (2 * ep + d) + c
                act.wait_ge(*filled("h", n))
                if n >= 4:
                    u0, c0 = divmod(n // 2 - 2, 2)
                    if c0:
                        act.wait_ge(*filled("e", u0))
                    else:
                        act.wait_ge(down_done, u0 + 1)
                b = n % 3
                A(HR[n % 4][:, :], PS[b][:, :], ACT.Gelu, bias=B1P[:, col:col + 1]).then_inc(bank_drained[b], 1)

            def high_half(t):
                j, r = divmod(t - 14, 4)
                if r == 0 and 0 <= j < NG:
                    act.wait_ge(*filled("x2", j))
                    A(X2[:, 512 * j:512 * j + 512], PS[6][:, :], ACT.Copy).then_inc(x2hi_ready, 1)

            def output_transposed(t):
                j, r = divmod(t - 10, 4)
                if r == 0 and 0 <= j < NG:
                    for half in range(2):
                        act.wait_ge(*filled("on", j, half))
                        if half == 0 and j >= 1:
                            act.wait_ge(*filled("y", j - 1))
                        for q in range(2):
                            src = PS[7 - 2 * half][:, 2 * q * P:2 * q * P + 2 * P]\
                                .rearrange("p (w g o) -> p g w o", w=2, g=2)
                            last = A(ONT[:, 2 * half + q, :, :].rearrange("p g (w o) -> p g w o", w=2), src, ACT.Copy)
                        last.then_inc(bank_drained[7 - 2 * half], 1)

            def spread_weights(t):
                j, r = divmod(t - 17, 4)
                if r == 0 and 0 <= j < NG:
                    act.wait_ge(*filled("gt", j))
                    A(GT[:, 512 * j:512 * j + 512], PS[6][0:24, 0:256].bitcast(BF16),
                      ACT.Copy).then_inc(bank_drained[6], 1)

            def router_tanh(t):
                j, r = divmod(t - 16, 4)
                if r == 0 and 0 <= j < NG:
                    act.wait_ge(arg_ready, j + 1)
                    A(PX[:, :, :], AR[:, :, :], ACT.Tanh).then_inc(tanh_ready, 1)

            for t in range(LAG + 4 * NG + 1):
                if t < NPAIR:
                    for tv in ([0, 1] if t == 0 else [t + 1]):
                        if tv >= NPAIR:
                            continue
                        if tv < 3:
                            act.wait_ge(bv_zeroed, tv + 1)
                        else:
                            act.wait_ge(*filled("o", tv - 3))
                        act.wait_ge(*filled("v", tv))
                        for w in range(2):
                            last = A(BV[tv % 3][w * C:w * C + C, :, w, 0:HD],
                                     PS[6][w * C:w * C + C, 0:256].rearrange("p (h d) -> p h d", h=NH), ACT.Copy)
                        last.then_inc(bank_drained[6], 1)
                        if t == 0 and tv == 0:
                            continue
                    act.wait_ge(*drained("score", t))
                    if t >= 2 and (t - 2) % 4 == 3:
                        act.wait_ge(*filled("ss", (t - 2) // 4))
                    elif t >= 2:
                        act.wait_ge(sq_used, t - 1 - (t - 1) // 4)
                    A(SQ[t % 2][:, :], SR[t % 3][:, :], ACT.Square).then_inc(sq_ready, 1)
                if 1 <= t <= NPAIR:
                    a = t - 1
                    if a == 0:
                        act.wait_ge(*filled("k", 1, NG - 1))
                    if a >= 8:
                        act.wait_ge(on_ready, a - 7)
                    act.wait_ge(*filled("o", a))
                    A(OR[:, a % 8, :, :, :].rearrange("p h w d -> p (h w d)"), PS[2 + a % 2][:, 0:264],
                      ACT.Copy).then_inc(bank_drained[2 + a % 2], 1)
                if 5 <= t and (t - 5) % 4 == 0 and (t - 5) // 4 < NG:
                    j = (t - 5) // 4
                    if j >= 1:
                        act.wait_ge(*filled("st", j - 1))
                    else:
                        act.wait_ge(*moved(5))
                    act.wait_ge(*filled("ss", j))
                    A(SSB[:, :], PS[4][:, :], ACT.Copy).then_inc(bank_drained[4], 1)
                if t < LAG:
                    output_transposed(t)
                if t < LAG:
                    high_half(t)
                for e in weight_steps(t):
                    if e % 4 == 0:
                        act.wait_ge(w1r_in, 32 * (e // 4 + 1))
                    A(W1H[:, e * HID:e * HID + HID], W1R[:, e % 4, :], ACT.Copy,
                      scale=LNG[:, e:e + 1]).then_inc(w1h_ready, 1)
                u = t - LAG
                if 0 <= u < 4 * NG:
                    if u == 0:
                        act.wait_ge(*filled("score", NPAIR - 1))
                        act.wait_ge(*drained("b1"))
                for n in range(4 * u, 4 * u + 4):
                    if n == 4 * u + 2:
                        if t >= LAG:
                            output_transposed(t)
                            high_half(t)
                        spread_weights(t)
                        router_tanh(t)
                    if 0 <= u < 4 * NG:
                        hidden_act(n)
                if 1 <= u <= 4 * NG:
                    if u >= 3:
                        act.wait_ge(*drained("e", u - 3))
                    act.wait_ge(*filled("gb", u - 1))
                    A(GB[(u - 1) % 2][:, :], PS[5][:, :], ACT.Copy).then_inc(bank_drained[5], 1)

        @block.vector
        def _(dve):
            n = [0]

            def step(ins):
                n[0] += 1
                ins.then_inc(dve_step, 1)
                dve.wait_ge(dve_step, n[0])

            V_ = nc.vector

            def inverse_root(y, v, work):
                step(V_.tensor_scalar(y.bitcast(I32), v.bitcast(I32), -0.5, float(0x5F3759DF), ALU.mult, ALU.add))
                for _ in range(3):
                    step(V_.scalar_tensor_tensor(out=work, in0=y, scalar=-0.5, in1=y, op0=ALU.mult, op1=ALU.mult))
                    step(V_.tensor_tensor(work, work, v, ALU.mult))
                    step(V_.scalar_tensor_tensor(out=y, in0=work, scalar=1.5, in1=y, op0=ALU.add, op1=ALU.mult))

            def moments(xin, j):
                for q in range(4):
                    last = V_.bn_stats(BNS[:, q, :], xin[:, q, :])
                step(last)
                for q in range(4):
                    last = V_.bn_aggr(MV[:, 4 * j + q, :], BNS[:, q, :])
                return last

            def normalise(dst, xin, root, j):
                for q in range(4):
                    last = V_.tensor_scalar(dst(q), xin(q), MV[:, 4 * j + q, 0:1], root(q), ALU.subtract, ALU.mult)
                return last

            V_.memset(BD[0][:, 0, 0:2, :], 0.0).then_inc(half_zeroed, 1)
            for j in range(NG):
                dve.wait_ge(x_in[j], 16)
                for q in range(4 * j, 4 * j + 4):
                    last = V_.bn_stats(BNX[:, q, :], XR[:, q, :])
            step(last)
            for q in range(NPAIR):
                last = V_.bn_aggr(MV[:, q, :], BNX[:, q, :])
            step(last)
            step(V_.tensor_scalar(VE[:, :], MV[:, :, 1], EPS_C, None, ALU.add))
            inverse_root(RS[:, :], VE[:, :], RA[:, :])
            V_.scalar_tensor_tensor(out=NB[:, :], in0=MV[:, :, 0], scalar=-1.0, in1=RS[:, :], op0=ALU.mult,
                                    op1=ALU.mult).then_inc(rx_ready, 1)
            for j in range(NDVE):
                normalise(lambda q: XN[:, 4 * j + q, :, :], lambda q: twice(XR[:, 4 * j + q, :]),
                          lambda q: RS[:, 4 * j + q:4 * j + q + 1], j).then_inc(xn_ready, 1)
            for j in range(NG):
                dve.wait_ge(xhi_ready, j + 1)
                lo = XS[C:P, 8 * j:8 * j + 8, :].rearrange("p w o -> p (w o)")
                b = before[("xt", j)][0]
                V_.tensor_tensor(lo, PS[b][C:P, :], lo.bitcast(F32), ALU.subtract).then_inc(bank_drained[b], 1)
            def dve_spread(dst, src, bias):
                return V_.tensor_scalar(dst, src, bias, None, ALU.add)

            dve.wait_ge(small_in, 16 * N_SMALL)
            spread_first(dve, dve_spread, range(2, 4))
            dve.wait_ge(b1_in, 16)
            dve.wait_ge(*filled("b1"))
            V_.tensor_tensor(B1P[:, :], PS[3][:, 0:16], B1[:, :], ALU.add).then_inc(bank_drained[3], 1)
            dve.wait_ge(wvh_ready, 1)
            V_.tensor_tensor(WVL[:, :], WS[:, V * 256:], WVH[:, :].bitcast(F32), ALU.subtract).then_inc(wvl_ready, 1)
            dve.wait_ge(wrh_ready, 1)
            V_.tensor_tensor(WRR[:, 1, :], WRs[:, :], WRR[:, 0, :].bitcast(F32), ALU.subtract).then_inc(wrr_ready, 1)
            for is_tile, c, i in stage_b():
                tile = 8 * c + i
                if not is_tile:
                    if tile in (1, 3):
                        stage(dve, dve_spread, 1, tile)
                    if tile == 4:
                        dve.wait_ge(rel0_in, 16)
                        for oj in range(WH):
                            src = RB[:, ::-1].rearrange("p (y c) -> p y c", c=SIDE)
                            last = V_.tensor_copy(EB[:, oj, :, :], src[:, :, WH - 1 - oj:2 * WH - 1 - oj])
                        last.then_inc(bias_rows, 1)
                    if c == 1 and i >= 4:
                        j = i - 4
                        b = i
                        dve.wait_ge(xchi_ready, j + 1)
                        lo = XC[C:P, 512 * j:512 * j + 512]
                        V_.tensor_tensor(lo, PS[b][C:P, :], lo.bitcast(F32),
                                         ALU.subtract).then_inc(bank_drained[b], 1)
                    continue
                if c < 2:
                    move_tn(dve, V_.tensor_copy, tile, 1)
                else:
                    i0 = 4 * (tile - 16)
                    if tile == 16:
                        dve.wait_ge(xb_ready, 1)
                        dve.wait_ge(bias_in, 16 * 16)
                        dve.wait_ge(*filled("t", 15))
                        dve.wait_ge(wvl_ready, 1)
                    dve.wait_ge(*filled("t", tile))
                    bias = BI[:, :, i0:i0 + 4].rearrange("p h i -> p i h").unsqueeze(3)
                    V_.tensor_tensor(TM[:, :, i0:i0 + 4].rearrange("p (h w) i -> p i h w", h=4),
                                     PS[tile % 4][:, :].rearrange("p (i h w) -> p i h w", i=4, h=4),
                                     bias.to_broadcast([P, 4, 4, NW]), ALU.add)\
                        .then_inc(bank_drained[tile % 4], 1)

            dve.wait_ge(*drained("t", 15))
            def score_variance(t):
                j, r = divmod(t - 6, 4)
                if r == 0 and 0 <= j < NG:
                    q0 = (4 * j) % 8
                    dve.wait_ge(*drained("o", 4 * j + 3))
                    sums = OR[:, q0:q0 + 4, :, :, HD].rearrange("p q h w -> p q (h w)")
                    step(V_.scalar_tensor_tensor(out=VA[:, :, :, :].rearrange("p q h w -> p q (h w)"), in0=sums,
                                                 scalar=-1.0 / WT, in1=sums, op0=ALU.mult, op1=ALU.mult))
                    if j >= 1:
                        dve.wait_ge(rsc_ready, j)
                    dve.wait_ge(*filled("st", j))
                    ss = PS[5][:, :].rearrange("p (h q r) -> p q h r", h=4, q=4)[:, :, :, 0:2]
                    V_.tensor_tensor(VB[:, :, :, :], ss, VA[:, :, :, :], ALU.add).then_inc(bank_drained[5], 1)

            for t in range(LAG + 4 * NG + 3):
                u = t - LAG - 2
                if 0 <= u < 4 * NG:
                    j, ep = divmod(u, 4)
                    if ep == 0 and j >= 2:
                        dve.wait_ge(*filled("out", j - 2))
                    dve.wait_ge(*drained("gb", u))
                    dve.wait_ge(*filled("e", u))
                    if u >= 2:
                        dve.wait_ge(gate_done, u - 1 - (u - 1) // 4)
                    b = 3 + u % 2
                    dst = AC[j % 2] if ep == 0 else GM
                    ins = V_.scalar_tensor_tensor(out=dst[:, :], in0=PS[b][:, :], scalar=B2[:, ep:ep + 1],
                                                  in1=GB[u % 2][:, :], op0=ALU.add, op1=ALU.mult)
                    ins.then_inc(bank_drained[b], 1)
                    if ep and u < 4 * NG - 1:
                        dve.wait_ge(*drained("e", u))
                        V_.tensor_tensor(AC[j % 2][:, :], AC[j % 2][:, :], GM[:, :], ALU.add).then_inc(gate_done, 1)
                j, r = divmod(t - LAG - 6, 4)
                if r == 0 and 0 <= j < NG:
                    y = XR[:, 4 * j:4 * j + 4, :]
                    dve.wait_ge(*filled("out", j))
                    parts = PS[6][:, :].rearrange("p (q d c) -> p q d c", q=4, d=2)
                    step(V_.tensor_tensor(y, parts[:, :, 0, :], y, ALU.add))
                    V_.tensor_tensor(y, parts[:, :, 1, :], y, ALU.add).then_inc(bank_drained[6], 1)
                if t < NPAIR:
                    if t == 0:
                        dve.wait_ge(*filled("t", 31))
                        dve.wait_ge(*moved(4))
                    if t == 2:
                        dve.wait_ge(*moved(5))
                    if t >= 3:
                        dve.wait_ge(*filled("o", t - 3))
                        dve.wait_ge(sq_ready, t - 2)
                    dve.wait_ge(*filled("score", t))
                    dst = SR[t % 3][:, :]
                    V_.tensor_tensor(dst, PS[t % 2][:, :], TN[:, t, :, :, :].rearrange("p h g o -> p (h g o)"),
                                     ALU.add).then_inc(bank_drained[t % 2], 1)
                score_variance(t)
                for e in weight_steps(t - 1):
                    dve.wait_ge(w1h_ready, e + 1)
                    cols = slice(e * HID, e * HID + HID)
                    V_.scalar_tensor_tensor(out=W1L[:, cols], in0=W1R[:, e % 4, :], scalar=LNG[:, e:e + 1],
                                            in1=W1H[:, cols].bitcast(F32), op0=ALU.mult,
                                            op1=ALU.subtract).then_inc(w1l_ready, 1)
                j, r = divmod(t - 9, 4)
                if r == 0 and 0 <= j < NG:
                    q0 = (4 * j) % 8
                    dve.wait_ge(rsc_ready, j + 1)
                    if j >= 1:
                        dve.wait_ge(*filled("on", j - 1, 0))
                        dve.wait_ge(*filled("on", j - 1, 1))
                    for q in range(4):
                        V_.tensor_tensor(ON[:, q, :, :, :].rearrange("p w h d -> p h w d"),
                                         OR[:, q0 + q, :, :, 0:HD],
                                         RSC[:, q, :, :].unsqueeze(3).to_broadcast([P, 4, 2, HD]),
                                         ALU.mult).then_inc(on_ready, 1)
                j, r = divmod(t - 16, 4)
                if r == 0 and 0 <= j < NG:
                    dve.wait_ge(tanh_ready, j + 1)
                    step(V_.scalar_tensor_tensor(out=PR[:, :, :], in0=PX[:, :, :], scalar=1.0, in1=PR[:, :, :],
                                                 op0=ALU.add, op1=ALU.mult))
                    if j >= 1:
                        dve.wait_ge(*filled("gt", j - 1))
                    step(V_.tensor_copy(G3[:, :, 0, :], PR[:, :, :]))
                    step(V_.tensor_tensor(PR[:, :, :], PR[:, :, :], G3[:, :, 0, :], ALU.subtract))
                    step(V_.tensor_copy(G3[:, :, 1, :], PR[:, :, :]))
                    V_.tensor_tensor(G3[:, :, 2, :], PR[:, :, :], G3[:, :, 1, :], ALU.subtract).then_inc(g3_ready, 1)
                j, r = divmod(t - 12, 4)
                if r == 0 and 0 <= j < NG:
                    x1 = XR[:, 4 * j:4 * j + 4, :]
                    dve.wait_ge(*filled("y", j))
                    V_.tensor_tensor(x1, PS[7][:, 0:256].rearrange("p (q c) -> p q c", q=4), x1,
                                     ALU.add).then_inc(bank_drained[7], 1)
                    dve.wait_ge(*drained("y", j))
                    moments(x1, j).then_inc(mv_ready, 1)
                j, r = divmod(t - 13, 4)
                if r == 0 and 0 <= j < NG:
                    dve.wait_ge(rz_ready, 3 * j + 1)
                    step(normalise(lambda q: Z[:, q, :], lambda q: XR[:, 4 * j + q, :],
                                   lambda q: RZ[:, 0, j, q:q + 1], j))
                    dve.wait_ge(rz_ready, 3 * j + 2)
                    if j >= 1:
                        dve.wait_ge(*filled("x2", j - 1))
                    V_.tensor_tensor(Z2[:, :, :, :], Z[:, :, :].unsqueeze(2).to_broadcast([P, 4, 2, C]),
                                     RZ[:, 1, j, :].unsqueeze(2).unsqueeze(3).to_broadcast([P, 4, 2, C]),
                                     ALU.mult).then_inc(z2_ready, 1)
                j, r = divmod(t - 14, 4)
                if r == 0 and 0 <= j < NG:
                    dve.wait_ge(x2hi_ready, j + 1)
                    lo = X2[C:P, 512 * j:512 * j + 512]
                    V_.tensor_tensor(lo, PS[6][C:P, :], lo.bitcast(F32), ALU.subtract).then_inc(bank_drained[6], 1)
                j, r = divmod(t - 15, 4)
                if r == 0 and 0 <= j < NG:
                    dve.wait_ge(*filled("lg", j))
                    parts = PS[6][:, 0:64].rearrange("p (q k e) -> p q k e", q=4, k=2)
                    step(V_.tensor_copy(LG[:, :, :], parts[:, :, 0, :]))
                    V_.tensor_tensor(LG[:, :, :], LG[:, :, :], parts[:, :, 1, :], ALU.add)\
                        .then_inc(bank_drained[6], 1)
                    dve.wait_ge(*drained("lg", j))
                    dve.wait_ge(rz_ready, 3 * j + 3)
                    step(V_.tensor_tensor(LG[:, :, :], LG[:, :, :],
                                          RZ[:, 2, j, :].unsqueeze(2).to_broadcast([P, 4, NE]), ALU.mult))
                    step(V_.tensor_tensor(LG[:, :, :], LG[:, :, :],
                                          BRB[:, :].unsqueeze(1).to_broadcast([P, 4, NE]), ALU.add))
                    step(V_.tensor_reduce(M1[:, :], LG[:, :, :], AX.X, ALU.max))
                    step(V_.tensor_tensor(LG[:, :, :], LG[:, :, :], M1[:, :].unsqueeze(2).to_broadcast([P, 4, NE]),
                                          ALU.subtract))
                    other = LG[:, :, :].unsqueeze(2).to_broadcast([P, 4, NE, NE])
                    own = LG[:, :, :].unsqueeze(3).to_broadcast([P, 4, NE, NE])
                    flat = lambda m: m[:, :, :, :].rearrange("p q e f -> p q (e f)")
                    step(V_.tensor_tensor(CG[:, :, :, :], other, own, ALU.subtract))
                    step(V_.scalar_tensor_tensor(out=flat(CE), in0=flat(CG), scalar=0.0,
                                                 in1=TRI[:, :, :].rearrange("p e f -> p (e f)").unsqueeze(1)
                                                 .to_broadcast([P, 4, NE * NE]),
                                                 op0=ALU.is_equal, op1=ALU.mult))
                    step(V_.scalar_tensor_tensor(out=flat(CG), in0=flat(CG), scalar=0.0, in1=flat(CE),
                                                 op0=ALU.is_gt, op1=ALU.add))
                    step(V_.tensor_reduce(PR[:, :, :], CG[:, :, :, :], AX.X, ALU.add))
                    step(V_.tensor_scalar(PR[:, :, :], PR[:, :, :], 1.5, 0.5, ALU.is_lt, ALU.mult))
                    step(V_.tensor_tensor(AR[:, :, :], PR[:, :, :], LG[:, :, :], ALU.mult))
                    step(V_.tensor_reduce(M1[:, :], AR[:, :, :], AX.X, ALU.add))
                    V_.tensor_tensor(AR[:, :, :], LG[:, :, :], M1[:, :].unsqueeze(2).to_broadcast([P, 4, NE]),
                                     ALU.subtract).then_inc(arg_ready, 1)



def kernel(**inputs):
    import numpy as np
    import concourse.bacc as bacc
    from concourse.bass_utils import run_bass_kernel_spmd

    a = {k: np.asarray(v) for k, v in inputs.items()}
    rel = a["L0_conv_intrinsic"].reshape(2, 4, NREL, 1 + 2 * HD)
    arrays = {
        "x": a["x"].reshape(2, 4, WH, 2, 2, WH, C).transpose(4, 2, 5, 0, 1, 3, 6).reshape(P, NPAIR, C),
        "W_prep": a["L0_conv_W_prep"],
        "b_prep": a["L0_conv_b_prep"].reshape(10, P).T,
        "rel": rel[..., 1:].reshape(2, 4, NREL, 2, HD).transpose(1, 4, 3, 0, 2).reshape(P, 2, 2, NREL),
        "rel0": rel[..., 0].reshape(NH, NREL),
        "W_fin": a["L0_conv_W_fin"].reshape(2, P, C).transpose(1, 0, 2),
        "b_fin": a["L0_conv_b_fin"],
        "Wr": a["L0_ffn_Wr"],
        "br": a["L0_ffn_br"],
        "ln_g": a["L0_ffn_ln_g"].T,
        "ln_b": a["L0_ffn_ln_b"].T,
        "W1": a["L0_ffn_W1"].transpose(1, 0, 2),
        "b1": a["L0_ffn_b1"].reshape(2 * NE, P).T,
        "W2": a["L0_ffn_W2"].reshape(2 * NE, P, C).transpose(1, 0, 2),
        "b2": a["L0_ffn_b2"].reshape(4, P).T,
    }
    arrays = {k: np.ascontiguousarray(v) for k, v in arrays.items()}
    nc = bacc.Bacc("TRN2", target_bir_lowering=False, num_devices=1)
    args = [nc.dram_tensor(f"in_{k}", v.shape, mybir.dt.from_np(v.dtype), kind="ExternalInput").ap()
            for k, v in arrays.items()]
    out = nc.dram_tensor("out", (P, NPAIR, C), F32, kind="ExternalOutput").ap()
    metaformer_kernel(nc, *args, out)
    r = run_bass_kernel_spmd(nc, [{f"in_{k}": v for k, v in arrays.items()}], core_ids=[0])
    y = np.asarray(r.results[0]["out"]).reshape(2, WH, WH, 2, 4, 2, C)
    return np.ascontiguousarray(y.transpose(3, 4, 1, 5, 0, 2, 6).reshape(2, 32, 32, C))
```
